# Optimizing a Trainium2 kernel written in Bass

```python
import numpy as np
import jax
import jax.numpy as jnp

def _softmax(x, axis=-1):
    return jax.nn.softmax(x, axis=axis)

def _gelu(x):
    return jax.nn.gelu(x, approximate=True)

def _silu(x):
    return jax.nn.silu(x)

def _sigmoid(x):
    return jax.nn.sigmoid(x)

def _layernorm(x, axis=-1, eps=1e-05):
    m = jnp.mean(x, axis=axis, keepdims=True)
    v = jnp.var(x, axis=axis, keepdims=True)
    return (x - m) / jnp.sqrt(v + eps)

def _scatter_add(tgt, idx, src, axis=0):
    return tgt.at[idx].add(src)

def _segment_sum(src, seg, n):
    return jax.ops.segment_sum(src, seg, n)
kernel_name = 'mk_recurrent_d2_jaxref_r8_94a98e'

def setup_inputs(seed: int=0):
    np.random.seed(seed)
    _w = jnp.asarray

    def _L0_attn_setup():
        import jax, jax.numpy as jnp
        import numpy as np
        D_MODEL = 128
        NUM_HEADS = 16
        D_K = D_MODEL // NUM_HEADS
        THETA = 10000.0

        def apply_rope(x, positions):
            half = D_K // 2
            inv_freq = THETA ** (-jnp.arange(half, dtype=jnp.float32) * 2.0 / D_K)
            angles = positions[:, None, :, None].astype(jnp.float32) * inv_freq
            cos, sin = (jnp.cos(angles), jnp.sin(angles))
            x1 = x[..., 0::2]
            x2 = x[..., 1::2]
            out_even = x1 * cos - x2 * sin
            out_odd = x1 * sin + x2 * cos
            out = jnp.stack([out_even, out_odd], axis=-1)
            return out.reshape(x.shape)
        key = jax.random.key(seed)
        ks = jax.random.split(key, 5)
        b, s = (2, 256)
        scale = 0.02
        return {'x': jax.random.normal(ks[0], (b, s, D_MODEL), dtype=jnp.float32), 'Wq': jax.random.normal(ks[1], (D_MODEL, D_MODEL), dtype=jnp.float32) * scale, 'Wk': jax.random.normal(ks[2], (D_MODEL, D_MODEL), dtype=jnp.float32) * scale, 'Wv': jax.random.normal(ks[3], (D_MODEL, D_MODEL), dtype=jnp.float32) * scale, 'Wo': jax.random.normal(ks[4], (D_MODEL, D_MODEL), dtype=jnp.float32) * scale}
    _L0_attn_in = _L0_attn_setup()

    def _L0_ffn_setup():
        import jax, jax.numpy as jnp
        import numpy as np
        B, S, H, E = (2, 1024, 128, 8)
        SCALE = 0.5
        key = jax.random.key(seed)
        k1, k2 = jax.random.split(key)
        x = jax.random.normal(k1, (B, S, H), dtype=jnp.float32)
        gate_w = jax.random.normal(k2, (E, H), dtype=jnp.float32) * 0.02
        coeff = SCALE * (1.0 + 0.05 * jnp.arange(E, dtype=jnp.float32))
        expert_w = coeff[:, None, None] * jnp.eye(H, dtype=jnp.float32)
        return {'x': x, 'gate_w': gate_w, 'expert_w': expert_w}
    _L0_ffn_in = _L0_ffn_setup()

    def _L1_attn_setup():
        import jax, jax.numpy as jnp
        import numpy as np
        import math
        B, S, HID, H = (2, 256, 128, 16)
        D = HID // H

        def _get_slopes(n):
            start = 2 ** (-2 ** (-(math.log2(n) - 3)))
            return np.array([start * 2 ** (-i) for i in range(n)], dtype=np.float32)
        key = jax.random.key(seed)
        ks = jax.random.split(key, 9)
        sc = 1.0 / math.sqrt(HID)
        return {'x': jax.random.normal(ks[0], (B, S, HID), dtype=jnp.float32), 'Wq': jax.random.normal(ks[1], (HID, HID), dtype=jnp.float32) * sc, 'bq': jnp.zeros((HID,), dtype=jnp.float32), 'Wk': jax.random.normal(ks[2], (HID, HID), dtype=jnp.float32) * sc, 'bk': jnp.zeros((HID,), dtype=jnp.float32), 'Wv': jax.random.normal(ks[3], (HID, HID), dtype=jnp.float32) * sc, 'bv': jnp.zeros((HID,), dtype=jnp.float32), 'Wo': jax.random.normal(ks[4], (HID, HID), dtype=jnp.float32) * sc, 'bo': jnp.zeros((HID,), dtype=jnp.float32), 'slopes': jnp.asarray(_get_slopes(H))}
    _L1_attn_in = _L1_attn_setup()

    def _L1_ffn_setup():
        import jax, jax.numpy as jnp
        import numpy as np
        TOP_K = 2
        key = jax.random.key(seed)
        k1, k2, k3, k4 = jax.random.split(key, 4)
        B, T, D, F, E = (2, 128, 128, 256, 8)
        x = jax.random.normal(k1, (B, T, D), dtype=jnp.float32)
        Wg = jax.random.normal(k2, (D, E), dtype=jnp.float32) * 0.02
        W1 = jax.random.normal(k3, (E, D, F), dtype=jnp.float32) * 0.02
        W2 = jax.random.normal(k4, (E, F, D), dtype=jnp.float32) * 0.02
        return {'x': x, 'Wg': Wg, 'W1': W1, 'W2': W2}
    _L1_ffn_in = _L1_ffn_setup()
    _d = {'L0_attn_x': _L0_attn_in['x'], 'L0_attn_Wq': _L0_attn_in['Wq'], 'L0_attn_Wk': _L0_attn_in['Wk'], 'L0_attn_Wv': _L0_attn_in['Wv'], 'L0_attn_Wo': _L0_attn_in['Wo'], 'L0_ffn_gate_w': _L0_ffn_in['gate_w'], 'L0_ffn_expert_w': _L0_ffn_in['expert_w'], 'L1_attn_Wq': _L1_attn_in['Wq'], 'L1_attn_bq': _L1_attn_in['bq'], 'L1_attn_Wk': _L1_attn_in['Wk'], 'L1_attn_bk': _L1_attn_in['bk'], 'L1_attn_Wv': _L1_attn_in['Wv'], 'L1_attn_bv': _L1_attn_in['bv'], 'L1_attn_Wo': _L1_attn_in['Wo'], 'L1_attn_bo': _L1_attn_in['bo'], 'L1_attn_slopes': _L1_attn_in['slopes'], 'L1_ffn_Wg': _L1_ffn_in['Wg'], 'L1_ffn_W1': _L1_ffn_in['W1'], 'L1_ffn_W2': _L1_ffn_in['W2']}
    _x0 = _d['L0_attn_x']
    _d['L0_attn_x'] = jax.random.normal(jax.random.fold_in(jax.random.key(seed), 1), (8, 512, 128), dtype=_x0.dtype)
    del _x0
    return _d

def reference(L0_attn_x, L0_attn_Wq, L0_attn_Wk, L0_attn_Wv, L0_attn_Wo, L0_ffn_gate_w, L0_ffn_expert_w, L1_attn_Wq, L1_attn_bq, L1_attn_Wk, L1_attn_bk, L1_attn_Wv, L1_attn_bv, L1_attn_Wo, L1_attn_bo, L1_attn_slopes, L1_ffn_Wg, L1_ffn_W1, L1_ffn_W2):

    def _L0_attn_ref(x, Wq, Wk, Wv, Wo):
        import jax, jax.numpy as jnp
        import numpy as np
        D_MODEL = 128
        NUM_HEADS = 16
        D_K = D_MODEL // NUM_HEADS
        THETA = 10000.0

        def apply_rope(x, positions):
            half = D_K // 2
            inv_freq = THETA ** (-jnp.arange(half, dtype=jnp.float32) * 2.0 / D_K)
            angles = positions[:, None, :, None].astype(jnp.float32) * inv_freq
            cos, sin = (jnp.cos(angles), jnp.sin(angles))
            x1 = x[..., 0::2]
            x2 = x[..., 1::2]
            out_even = x1 * cos - x2 * sin
            out_odd = x1 * sin + x2 * cos
            out = jnp.stack([out_even, out_odd], axis=-1)
            return out.reshape(x.shape)
        b, s, _ = x.shape
        Q = x @ Wq.T
        K = x @ Wk.T
        V = x @ Wv.T
        split = lambda t: t.reshape(b, s, NUM_HEADS, D_K).transpose(0, 2, 1, 3)
        Q, K, V = (split(Q), split(K), split(V))
        positions = jnp.broadcast_to(jnp.arange(s, dtype=jnp.int32), (b, s))
        Q = apply_rope(Q, positions)
        K = apply_rope(K, positions)
        scores = jnp.einsum('bhqd,bhkd->bhqk', Q, K) / jnp.sqrt(jnp.float32(D_K))
        causal = jnp.tril(jnp.ones((s, s), dtype=bool))
        scores = jnp.where(causal[None, None], scores, -jnp.inf)
        attn = jax.nn.softmax(scores, axis=-1)
        out = jnp.einsum('bhqk,bhkd->bhqd', attn, V)
        out = out.transpose(0, 2, 1, 3).reshape(b, s, D_MODEL)
        return out @ Wo.T

    def _L0_ffn_ref(x, gate_w, expert_w):
        import jax, jax.numpy as jnp
        import numpy as np
        B, S, H, E = (2, 1024, 128, 8)
        SCALE = 0.5
        scores = jnp.einsum('bsh,eh->bse', x, gate_w)
        chosen = jnp.argmax(scores, axis=-1)
        onehot = jax.nn.one_hot(chosen, gate_w.shape[0], dtype=x.dtype)
        expert_out = jnp.einsum('bsh,efh->bsef', x, expert_w)
        return x + jnp.einsum('bsef,bse->bsf', expert_out, onehot)

    def _L1_attn_ref(x, Wq, bq, Wk, bk, Wv, bv, Wo, bo, slopes):
        import jax, jax.numpy as jnp
        import numpy as np
        import math
        B, S, HID, H = (2, 256, 128, 16)
        D = HID // H

        def _get_slopes(n):
            start = 2 ** (-2 ** (-(math.log2(n) - 3)))
            return np.array([start * 2 ** (-i) for i in range(n)], dtype=np.float32)
        b, s, hid = x.shape
        h = slopes.shape[0]
        d = hid // h
        q = (x @ Wq.T + bq).reshape(b, s, h, d).transpose(0, 2, 1, 3)
        k = (x @ Wk.T + bk).reshape(b, s, h, d).transpose(0, 2, 1, 3)
        v = (x @ Wv.T + bv).reshape(b, s, h, d).transpose(0, 2, 1, 3)
        scores = jnp.einsum('bhqd,bhkd->bhqk', q, k) / jnp.sqrt(jnp.float32(d))
        pos = jnp.arange(s)
        dist = (pos[None, :] - pos[:, None]).astype(x.dtype)
        scores = scores + slopes[None, :, None, None] * dist[None, None]
        attn = jax.nn.softmax(scores, axis=-1)
        ctx = jnp.einsum('bhqk,bhkd->bhqd', attn, v)
        ctx = ctx.transpose(0, 2, 1, 3).reshape(b, s, hid)
        return ctx @ Wo.T + bo

    def _L1_ffn_ref(x, Wg, W1, W2):
        import jax, jax.numpy as jnp
        import numpy as np
        TOP_K = 2
        B, T, D = x.shape
        E = Wg.shape[-1]
        xt = x.reshape(B * T, D)
        logits = xt @ Wg
        probs = jax.nn.softmax(logits, axis=-1)
        topw, topi = jax.lax.top_k(probs, TOP_K)
        topw = topw / jnp.sum(topw, axis=-1, keepdims=True)
        combine = jnp.sum(jax.nn.one_hot(topi, E, dtype=xt.dtype) * topw[..., None], axis=1)
        h = jax.nn.relu(jnp.einsum('nd,edf->enf', xt, W1))
        y = jnp.einsum('enf,efd->end', h, W2)
        out = jnp.einsum('ne,end->nd', combine, y)
        return out.reshape(B, T, D)
    x = L0_attn_x
    xn = _layernorm(x, axis=-1)
    s = _L0_attn_ref(xn, L0_attn_Wq, L0_attn_Wk, L0_attn_Wv, L0_attn_Wo)
    g = _silu(_L0_ffn_ref(xn, L0_ffn_gate_w, L0_ffn_expert_w))
    x = x + s * g
    xn = _layernorm(x, axis=-1)
    s = _L1_attn_ref(xn, L1_attn_Wq, L1_attn_bq, L1_attn_Wk, L1_attn_bk, L1_attn_Wv, L1_attn_bv, L1_attn_Wo, L1_attn_bo, L1_attn_slopes)
    g = _silu(_L1_ffn_ref(xn, L1_ffn_Wg, L1_ffn_W1, L1_ffn_W2))
    x = x + s * g
    return x

_drawn_inputs = setup_inputs


def setup_inputs(seed=0):
    import zlib

    import numpy as np

    out = dict(_drawn_inputs(seed))
    spreads = {'L1_attn_bq': (0.0, 0.8),
     'L1_attn_bk': (0.0, 0.8),
     'L1_attn_bv': (0.0, 0.8),
     'L1_attn_bo': (0.0, 0.8)}
    factors = {'L0_attn_Wq': 8.0,
     'L0_attn_Wk': 8.0,
     'L0_attn_Wv': 8.0,
     'L0_attn_Wo': 8.0,
     'L0_ffn_gate_w': 8.0,
     'L0_ffn_expert_w': 8.0,
     'L1_attn_Wq': 8.0,
     'L1_attn_Wk': 8.0,
     'L1_attn_Wv': 8.0,
     'L1_attn_Wo': 8.0,
     'L1_attn_slopes': 8.0,
     'L1_ffn_Wg': 8.0,
     'L1_ffn_W1': 8.0,
     'L1_ffn_W2': 8.0}
    for name, (base, spread) in spreads.items():
        noise = np.random.default_rng([zlib.crc32(name.encode()), seed]).standard_normal(out[name].shape)
        drawn = base * np.exp(spread * noise) if base else spread * noise
        out[name] = jnp.asarray(drawn.astype(out[name].dtype))
    for name, factor in factors.items():
        out[name] = (out[name] * factor).astype(out[name].dtype)
    return out
```

```python
from contextlib import ExitStack

import concourse.bass as bass
from concourse import mybir

F32 = mybir.dt.float32
BF16 = mybir.dt.bfloat16
ALU = mybir.AluOpType
ACT = mybir.ActivationFunctionType
AX = mybir.AxisListType

P = 128
BATCH, SEQ, D = 8, 512, 128
HEADS, DK = 16, 8
PAIRS, GROUPS = HEADS // 2, HEADS // 4
NBLK = SEQ // P
E = 8
F = 256
NF = F // P
LAYERS = (0, 1)
EPS = 1e-5
INV_SQRT_DK = 1.0 / float(DK) ** 0.5
MASKED = -1e30
TERMS = [(0, 0), (0, 1), (0, 2), (1, 0), (1, 1), (2, 0)]
PROD_ROWS = DK * len(TERMS)
BIAS_ROWS = (0, 6)
SCORE_ROWS = tuple(PROD_ROWS + n for n in BIAS_ROWS)
ALL_ROWS = tuple(n + 3 for n in SCORE_ROWS)
VW = 32


def spread(*lanes):
    keyed = [((i + 0.5) / len(lane), n, s) for n, lane in enumerate(lanes) for i, s in enumerate(lane)]
    return [s for _, _, s in sorted(keyed, key=lambda t: (t[0], t[1]))]


def ffn_steps(l, e):
    if l == 0:
        return [("bc", 0, e), ("y0", 0, e)]
    return [("bc", 1, e)] + [("h", 1, e, f) for f in range(NF)] + [("y1", 1, e, f) for f in range(NF)]


def layer_steps(l):
    steps = [("xnT", l)]
    steps += [("proj", l, n) for n in (("q", "qr", "k", "kr") if l == 0 else ("q", "k"))]
    steps += [("gate", l), ("v", l), ("ohT", l)]
    early = 4 if l == 0 else 2
    for e in range(early):
        steps += ffn_steps(l, e)
    late = list(range(early, E))
    fill = {0: 0, 1: 0}
    fill = {i: [] for i in range(PAIRS + 4)}
    spots = ([8, 9, 10, 11] if l == 0 else [0, 1, 8, 9, 10, 11])
    for e, i in zip(late, spots):
        fill[i] += ffn_steps(l, e)
    for i in range(PAIRS + 4):
        first = [("s", l, i, j, qb) for j in range(2) for qb in range(NBLK)] if i < PAIRS else []
        if 1 <= i <= PAIRS:
            first.insert(min(3, len(first)), ("mT", l, i - 1))
        second = [("st", l, i - 2, j, kb) for j in range(2) for kb in range(NBLK)] if 2 <= i < PAIRS + 2 else []
        pv = []
        if i >= 4:
            g = (i - 4) // 2
            pv = [("pv", l, g, kb) for kb in ((0, 1) if i % 2 == 0 else (2, 3))]
        steps += spread(first, second, pv, fill[i])
    steps += [("silu", l), ("wo", l), ("xT", l)]
    return steps


STEPS = layer_steps(0) + layer_steps(1)
W_KINDS = ("xnT", "proj", "gate", "v", "ohT", "bc", "h", "mT", "wo", "xT")
W_USE = {s: n for n, s in enumerate(t for t in STEPS if t[0] in W_KINDS)}
S_USE = {s: n for n, s in enumerate(t for t in STEPS if t[0] == "s")}
T_USE = {s: n for n, s in enumerate(t for t in STEPS if t[0] == "st")}
assert len(W_USE) % 2 == 0 and len(S_USE) % 2 == 0 and len(T_USE) % 2 == 0


class Turn:

    def __init__(self, eng, batch):
        self.eng, self.batch, self.bases, self.waits = eng, batch, {}, 0
        self.scratch = [eng.alloc_register(f"wait_value{i}") for i in range(8)]

    def value(self, per, k):
        if per not in self.bases:
            self.bases[per] = self.eng.alloc_register(f"batch_times_{per}")
            self.eng.reg_mul(self.bases[per], self.batch, per)
        reg = self.scratch[self.waits % len(self.scratch)]
        self.waits += 1
        self.eng.reg_add(reg, self.bases[per], k)
        return reg


class Signal:

    def __init__(self, ctx, nc, name, per=1, credit=0):
        self.sem = ctx.enter_context(nc.semaphore(name))
        self.per, self.credit = per, credit

    def __call__(self, b, k=1):
        return self.sem, b.value(self.per, self.credit + k)


class Ring:

    def __init__(self, ctx, nc, name, uses):
        self.banks = [ctx.enter_context(nc.psum_tensor(f"{name}{i}", [P, SEQ], F32)) for i in range(2)]
        self.full = [Signal(ctx, nc, f"{name}_full{i}", len(uses) // 2) for i in range(2)]
        self.free = [Signal(ctx, nc, f"{name}_free{i}", len(uses) // 2, credit=1) for i in range(2)]
        self.uses = uses

    def bank(self, step):
        return self.banks[self.uses[step] % 2]

    def filled(self, b, step):
        n = self.uses[step]
        return self.full[n % 2](b, n // 2 + 1)

    def freed(self, b, step):
        n = self.uses[step]
        return self.free[n % 2](b, n // 2)

    def emptied(self, b, step):
        n = self.uses[step]
        return self.free[n % 2](b, n // 2 + 1)

    def full_sem(self, step):
        return self.full[self.uses[step] % 2].sem

    def free_sem(self, step):
        return self.free[self.uses[step] % 2].sem


def two_layer_kernel(nc, x, wq0, wq0r, wk0, wk0r, wv0, wo0, gate0, expert0, wq1, wk1, wv1, wo1, gate1, w1, w2,
                     bq1, bk1, bv1, bo1, slopes, cos_t, sin_t, ident, causal, rank, select, key_rows, out):
    ctx = ExitStack()
    with ctx:
        def sb(name, shape, dt=F32):
            return ctx.enter_context(nc.sbuf_tensor(name, shape, dt))

        def sig(name, per=1, credit=0):
            return Signal(ctx, nc, name, per, credit)

        proj_w = {(0, "q"): sb("wq0_s", [P, D]), (0, "qr"): sb("wq0r_s", [P, D]), (0, "k"): sb("wk0_s", [P, D]),
                  (0, "kr"): sb("wk0r_s", [P, D]), (1, "q"): sb("wq1_s", [P, D]), (1, "k"): sb("wk1_s", [P, D])}
        wv_s = [sb("wv0_s", [P, D]), sb("wv1_s", [P, D])]
        wo_s = [sb("wo0_s", [P, D]), sb("wo1_s", [P, D])]
        gate_s = [sb("gate0_s", [P, E]), sb("gate1_s", [P, E])]
        expert_s = sb("expert_s", [P, E, D])
        w1_s = sb("w1_s", [P, E, F])
        w2_s = sb("w2_s", [P, E, NF, D])
        bq_s, bk_s, bo_s = sb("bq_s", [P, 1]), sb("bk_s", [P, 1]), sb("bo_s", [P, 1])
        bv_s = sb("bv_s", [P, D])
        cos_s, sin_s = sb("cos_s", [P, SEQ]), sb("sin_s", [P, SEQ])
        ident_s, identb_s = sb("ident_s", [P, P]), sb("identb_s", [P, P], BF16)
        causalb_s = sb("causalb_s", [P, P], BF16)
        rank_s = sb("rank_s", [P, NBLK, E])
        selectb_s = sb("selectb_s", [3 * E, E, P], BF16)
        slope_s, slope3_s = sb("slope_s", [HEADS, 4]), sb("slope3_s", [HEADS, 3], BF16)
        neg_half = sb("neg_half", [P, NBLK])

        x_s = [sb("x_in", [P, NBLK, D]), sb("x_mid", [P, NBLK, D])]
        x_out = sb("x_out", [P, NBLK, D])
        ln_stat = [sb(f"ln_stat{l}", [P, NBLK, 6]) for l in LAYERS]
        ln_mv = [sb(f"ln_mv{l}", [P, NBLK, 2]) for l in LAYERS]
        ln_var = [sb(f"ln_var{l}", [P, NBLK]) for l in LAYERS]
        ln_rstd = [sb(f"ln_rstd{l}", [P, NBLK]) for l in LAYERS]
        xn = sb("xn", [P, NBLK, D])
        xnT = [sb(f"xnT{l}", [P, SEQ]) for l in LAYERS]
        rope_a = {n: sb(f"rope_a_{n}", [P, SEQ]) for n in "qk"}
        rope_b = {n: sb(f"rope_b_{n}", [P, SEQ]) for n in "qk"}
        full = {n: sb(f"full_{n}", [P, SEQ]) for n in "qk"}
        rest = rope_a
        parts = {n: sb(f"parts_{n}", [P, 3, SEQ], BF16) for n in "qk"}
        ext = {(l, n): sb(f"ext_{n}{l}", [P, PAIRS, SEQ], BF16) for l in LAYERS for n in "qk"}
        v_ext = [sb(f"v_ext{l}", [P, NBLK, HEADS, VW]) for l in LAYERS]
        neg_max = [sb(f"neg_max{i}", [P, 2, NBLK]) for i in range(2)]
        neg_rest = [sb(f"neg_rest{i}", [P, 2, NBLK]) for i in range(2)]
        neg3 = [sb(f"neg3_{i}", [P, 2, 3, NBLK], BF16) for i in range(2)]
        neg_row = [sb(f"neg_row{i}", [2 * 3 * NBLK, P], BF16) for i in range(2)]
        probs = [sb(f"probs{i}", [P, 4, NBLK, SEQ]) for i in range(2)]
        stage = probs[1][:].rearrange("p m k n -> p (m k n)")
        select_s = stage[0:3 * E, 0:E * P].rearrange("p (e n) -> p e n", e=E)
        keyrow_s = stage[0:9, 1024:1536]
        keyrowb_s = stage[0:9, 1536:3584].bitcast(BF16).rearrange("p (h n) -> p h n", h=PAIRS)
        sloperow_s = stage[0:HEADS, 3584:4352].bitcast(BF16).rearrange("p (a n) -> p a n", a=3)
        causal_s = stage[:, 4352:4352 + P]
        o_quad = [sb(f"o_quad{i}", [P, SEQ]) for i in range(2)]
        o_heads = sb("o_heads", [P, SEQ])
        o_den = sb("o_den", [P, SEQ])
        lg = {n: sb(f"g_{n}", [P, NBLK, E]) for n in
              ("logit", "eq", "val", "oh1", "oh2", "shift", "exp", "prob", "prob2", "both", "comb", "rem")}
        lgs = {n: sb(f"gs_{n}", [P, NBLK]) for n in
               ("max", "vmax", "sum", "rsum", "max2", "vmax2", "csum", "rcsum")}
        onehot_b = sb("onehot_b", [P, NBLK, E], BF16)
        comb3_b = sb("comb3_b", [P, NBLK, 3, E], BF16)
        ohT = [sb("ohT0", [E, SEQ], BF16), sb("ohT1", [3 * E, SEQ], BF16)]
        x_e = [sb(f"x_e{i}", [P, SEQ]) for i in range(2)]
        hid = [sb(f"hid{i}", [P, SEQ]) for i in range(4)]
        y_s, y_sig, g_s = (sb(n, [P, SEQ]) for n in ("y_s", "y_sig", "g_s"))

        W = Ring(ctx, nc, "work", W_USE)
        S = Ring(ctx, nc, "score", S_USE)
        T = Ring(ctx, nc, "scoreT", T_USE)
        o_ps = ctx.enter_context(nc.psum_tensor("o_ps", [P, SEQ], F32))
        y_ps = ctx.enter_context(nc.psum_tensor("y_ps", [P, SEQ], F32))

        def per_layer(name, per=1):
            return [sig(f"{name}_{l}", per) for l in LAYERS]

        consts_in = sig("consts_in", 0)
        consts_cast = sig("consts_cast", 0)
        slope_step = sig("slope_step", 0)
        pool_consts = sig("pool_consts", 0)
        static_rows = sig("static_rows", 0)
        x_loaded = sig("x_loaded", 16)
        stat_done, aggr_done = per_layer("stat_done", NBLK), per_layer("aggr_done", NBLK)
        var_done, rstd_done, xn_done = per_layer("var_done"), per_layer("rstd_done"), per_layer("xn_done")
        full_done = sig("full_done", 2)
        hi_done, rest_done, mid_done, lo_done = (per_layer(n, 2) for n in ("hi_done", "rest_done", "mid_done", "lo_done"))
        ext_done = {(l, n): sig(f"ext_done_{n}{l}", 16 * 12) for l in LAYERS for n in "qk"}
        GATE_OPS = (5, 25)
        gate_step = [sig(f"gate_step_{l}", GATE_OPS[l]) for l in LAYERS]
        gate_exp = sig("gate_exp")
        xe_used = sig("xe_used", E)
        hid_used = sig("hid_used", E * NF)
        neg_step = per_layer("neg_step", 4 * PAIRS)
        mrow_in = [[sig(f"mrow_in{l}_{i}", 32 * PAIRS // 2) for i in range(2)] for l in LAYERS]
        mask_done = sig("mask_done", HEADS * NBLK)
        pv_done = per_layer("pv_done", GROUPS)
        o_out = per_layer("o_out", GROUPS)
        o_moved = [[sig(f"o_moved{l}_{i}", 16 * 8 * GROUPS // 2) for i in range(2)] for l in LAYERS]
        norm_step = per_layer("norm_step", 2)
        silu_sum, silu_exp, silu_step = sig("silu_sum"), per_layer("silu_exp"), per_layer("silu_step", 3)
        out_stored = sig("out_stored", 16, credit=16)

        LOADS = [(proj_w[0, "q"], wq0), (proj_w[0, "qr"], wq0r), (proj_w[0, "k"], wk0), (proj_w[0, "kr"], wk0r),
                 (proj_w[1, "q"], wq1), (proj_w[1, "k"], wk1), (wv_s[0], wv0), (wv_s[1], wv1), (wo_s[0], wo0),
                 (wo_s[1], wo1), (gate_s[0], gate0), (gate_s[1], gate1), (expert_s, expert0), (w1_s, w1),
                 (w2_s, w2), (bq_s, bq1), (bk_s, bk1), (bv_s, bv1), (bo_s, bo1), (cos_s, cos_t), (sin_s, sin_t),
                 (ident_s, ident), (rank_s, rank)]
        LOADS = [(t[:], src) for t, src in LOADS] + [(causal_s, causal), (select_s, select), (keyrow_s, key_rows)]
        N_LOADS = 16 * (len(LOADS) + 1)
        N_STATIC = 16 * (2 + 2 + 12)

        def side(j, rows=0):
            return slice(64 * j, 64 * j + rows)

        def w0(l, qb):
            return P * (qb + 1) if l == 0 else SEQ

        def q0(l, kb):
            return P * kb if l == 0 else 0

        block = ctx.enter_context(nc.Block())

        @block.sync
        def _(sp):
            for dst, src in LOADS:
                sp.dma_start(dst, src).then_inc(consts_in.sem, 16)
            sp.dma_start(slope_s[:, 0:1], slopes).then_inc(consts_in.sem, 16)
            sp.wait_ge(consts_cast.sem, 5)
            for j in range(2):
                sp.dma_start(ext[1, "k"][64 * j + PROD_ROWS:64 * j + ALL_ROWS[1]], keyrowb_s[0:9]).then_inc(static_rows.sem, 16)
                sp.dma_start(ext[0, "k"][64 * j + PROD_ROWS:64 * j + ALL_ROWS[0]], keyrowb_s[6:9]).then_inc(static_rows.sem, 16)
            sp.wait_ge(slope_step.sem, 6)
            for j in range(2):
                for n in range(6):
                    r = 64 * j + PROD_ROWS + n
                    sp.dma_start(ext[1, "q"][r:r + 1], sloperow_s[PAIRS * j:PAIRS * (j + 1), n % 3, :]).then_inc(static_rows.sem, 16)

            with sp.Fori(0, BATCH) as batch:
                b = Turn(sp, batch)
                sp.dma_start(x_s[0][:], x[batch]).then_inc(x_loaded.sem, 16)
                for step in STEPS:
                    kind, l = step[0], step[1]
                    if kind == "gate":
                        for i, n in enumerate("qk"):
                            sp.wait_ge(*lo_done[l](b, i + 1))
                            for j in range(2):
                                for t, term in enumerate(TERMS):
                                    r = 64 * j + DK * t
                                    sp.dma_start(ext[l, n][r:r + DK], parts[n][64 * j:64 * j + 64, term[i], :])\
                                      .then_inc(ext_done[l, n].sem, 16)
                    if kind == "mT":
                        p = step[2]
                        sp.wait_ge(*W.emptied(b, step))
                        for j in range(2):
                            r = 64 * j + SCORE_ROWS[l]
                            sp.dma_start(ext[l, "q"][r:r + 3, p, :].rearrange("r (k n) -> r k n", k=NBLK),
                                         neg_row[p % 2][12 * j:12 * j + 12, :]).then_inc(mrow_in[l][p % 2].sem, 16)
                    if kind == "pv" and step[3] == NBLK - 1:
                        g = step[2]
                        waits = [o_out[l](b, g + 1)]
                        if g == 0 and l == 1:
                            waits.append(W.emptied(b, ("xT", 0)))
                        for wait in waits:
                            sp.wait_ge(*wait)
                        for m in range(4):
                            to = slice(32 * m + DK * g, 32 * m + DK * g + DK)
                            sp.dma_start(o_heads[to], o_quad[g % 2][32 * m:32 * m + DK]).then_inc(o_moved[l][g % 2].sem, 16)
                            sp.dma_start(o_den[to], o_quad[g % 2][32 * m + DK:32 * m + 2 * DK]).then_inc(o_moved[l][g % 2].sem, 16)
                finished = W.emptied(b, ("xT", 1))
                sp.wait_ge(consts_in.sem, N_LOADS)
                sp.wait_ge(*finished)
                sp.dma_start(out[batch], x_out[:]).then_inc(out_stored.sem, 16)
            sp.wait_ge(out_stored.sem, out_stored.credit + 16 * BATCH)

        @block.tensor
        def _(pe):
            pe.wait_ge(consts_in.sem, N_LOADS)
            pe.wait_ge(consts_cast.sem, 5)
            pe.wait_ge(static_rows.sem, N_STATIC)
            pe.wait_ge(pool_consts.sem, 2)
            with pe.Fori(0, BATCH) as batch:
                b = Turn(pe, batch)
                for step in STEPS:
                    kind, l = step[0], step[1]
                    if kind in W_KINDS:
                        bank = W.bank(step)
                        bank_b = bank[:].bitcast(BF16)
                    if kind == "xnT":
                        pe.wait_ge(*xn_done[l](b))
                        pe.wait_ge(*W.freed(b, step))
                        for k in range(NBLK):
                            mm = pe.transpose(bank[:, P * k:P * k + P], xn[:, k, :], ident_s[:])
                        mm.then_inc(W.full_sem(step), 1)
                    elif kind == "proj":
                        pe.wait_ge(*W.emptied(b, ("xnT", l)))
                        pe.wait_ge(*W.freed(b, step))
                        pe.matmul(bank[:], proj_w[l, step[2]][:], xnT[l][:], start=True, stop=True)\
                          .then_inc(W.full_sem(step), 1)
                    elif kind == "gate":
                        pe.wait_ge(*W.freed(b, step))
                        for k in range(NBLK):
                            mm = pe.matmul(bank[:, E * k:E * k + E], xnT[l][:, P * k:P * k + P], gate_s[l][:],
                                           start=True, stop=True)
                        mm.then_inc(W.full_sem(step), 1)
                    elif kind == "v":
                        pe.wait_ge(*W.freed(b, step))
                        for k in range(NBLK):
                            mm = pe.matmul(bank[:, P * k:P * k + P], xnT[l][:, P * k:P * k + P], wv_s[l][:],
                                           start=True, stop=True)
                        mm.then_inc(W.full_sem(step), 1)
                    elif kind == "ohT":
                        pe.wait_ge(*gate_step[l](b, GATE_OPS[l]))
                        pe.wait_ge(*W.freed(b, step))
                        rows = ohT[l].shape[0]
                        for k in range(NBLK):
                            src = onehot_b[:, k, :] if l == 0 else comb3_b[:, k, :, :].rearrange("p a e -> p (a e)")
                            mm = pe.transpose(bank_b[0:rows, P * k:P * k + P], src, identb_s[:])
                        mm.then_inc(W.full_sem(step), 1)
                    elif kind == "bc":
                        e = step[2]
                        pe.wait_ge(*W.emptied(b, ("ohT", l)))
                        pe.wait_ge(*W.freed(b, step))
                        rows = ohT[l].shape[0]
                        pe.matmul(bank[:], selectb_s[0:rows, e, :], ohT[l][:], start=True, stop=True)\
                          .then_inc(W.full_sem(step), 1)
                    elif kind == "y0":
                        e = step[2]
                        pe.wait_ge(*W.emptied(b, ("bc", 0, e)))
                        mm = pe.matmul(y_ps[:], expert_s[:, e, :], x_e[e % 2][:], start=e == 0, stop=e == E - 1)
                        mm.then_inc(xe_used.sem, 1)
                    elif kind == "h":
                        e, f = step[2:]
                        pe.wait_ge(*W.emptied(b, ("bc", 1, e)))
                        pe.wait_ge(*W.freed(b, step))
                        mm = pe.matmul(bank[:], w1_s[:, e, P * f:P * f + P], x_e[e % 2][:], start=True, stop=True)
                        mm.then_inc(W.full_sem(step), 1)
                    elif kind == "y1":
                        e, f = step[2:]
                        pe.wait_ge(*W.emptied(b, ("h", 1, e, f)))
                        mm = pe.matmul(y_ps[:], w2_s[:, e, f, :], hid[(e * NF + f) % 4][:],
                                       start=e == 0 and f == 0, stop=e == E - 1 and f == NF - 1)
                        mm.then_inc(hid_used.sem, 1)
                    elif kind == "s":
                        p, j, qb = step[2:]
                        if p == 0 and j == 0 and qb == 0:
                            for n in "qk":
                                pe.wait_ge(*ext_done[l, n](b, 16 * 12))
                        pe.wait_ge(*S.freed(b, step))
                        rows, n = slice(64 * j, 64 * j + SCORE_ROWS[l]), w0(l, qb)
                        mm = pe.matmul(S.bank(step)[:, 0:n], ext[l, "q"][rows, p, P * qb:P * qb + P],
                                       ext[l, "k"][rows, p, 0:n], start=True, stop=l == 1)
                        if l == 0:
                            mm = pe.matmul(S.bank(step)[:, P * qb:n], identb_s[:], causalb_s[:], start=False, stop=True)
                        mm.then_inc(S.full_sem(step), 1)
                    elif kind == "mT":
                        p = step[2]
                        pe.wait_ge(*neg_step[l](b, 4 * p + 4))
                        pe.wait_ge(*W.freed(b, step))
                        pe.transpose(bank_b[0:24, 0:P], neg3[p % 2][:].rearrange("p j a k -> p (j a k)"), identb_s[:])\
                          .then_inc(W.full_sem(step), 1)
                    elif kind == "st":
                        p, j, kb = step[2:]
                        if j == 0 and kb == 0:
                            pe.wait_ge(*mrow_in[l][p % 2](b, 32 * (p // 2 + 1)))
                        pe.wait_ge(*T.freed(b, step))
                        rows, n = slice(64 * j, 64 * j + ALL_ROWS[l]), q0(l, kb)
                        pe.matmul(T.bank(step)[:, n:SEQ], ext[l, "k"][rows, p, P * kb:P * kb + P],
                                  ext[l, "q"][rows, p, n:SEQ], start=True, stop=True).then_inc(T.full_sem(step), 1)
                    elif kind == "pv":
                        g, kb = step[2:]
                        if l == 0:
                            pe.wait_ge(*mask_done(b, HEADS * g + 3 * NBLK + kb + 1))
                        else:
                            pe.wait_ge(*T.emptied(b, ("st", 1, 2 * g + 1, 1, kb)))
                        if kb == 0:
                            pe.wait_ge(*W.emptied(b, ("v", l)))
                            if g > 0:
                                pe.wait_ge(*o_out[l](b, g))
                        n = q0(l, kb)
                        for m in range(4):
                            mm = pe.matmul(o_ps[32 * m:32 * m + VW, n:SEQ], v_ext[l][:, kb, 4 * g + m, :],
                                           probs[g % 2][:, m, kb, n:SEQ], start=kb == 0, stop=kb == NBLK - 1)
                        if kb == NBLK - 1:
                            mm.then_inc(pv_done[l].sem, 1)
                    elif kind == "wo":
                        pe.wait_ge(*norm_step[l](b, 2))
                        pe.wait_ge(*W.freed(b, step))
                        pe.matmul(bank[:], wo_s[l][:], o_heads[:], start=True, stop=True).then_inc(W.full_sem(step), 1)
                    elif kind == "xT":
                        pe.wait_ge(*W.emptied(b, ("wo", l)))
                        pe.wait_ge(*W.freed(b, step))
                        for k in range(NBLK):
                            mm = pe.transpose(bank[:, P * k:P * k + P], g_s[:, P * k:P * k + P], ident_s[:])
                        mm.then_inc(W.full_sem(step), 1)

        @block.scalar
        def _(act):
            act.wait_ge(consts_in.sem, N_LOADS)
            act.wait_ge(consts_cast.sem, 5)
            act.wait_ge(static_rows.sem, N_STATIC)
            with act.Fori(0, BATCH) as batch:
                b = Turn(act, batch)
                for step in STEPS:
                    kind, l = step[0], step[1]
                    if kind == "xnT":
                        act.wait_ge(*W.filled(b, step))
                        nc.scalar.copy(xnT[l][:], W.bank(step)[:]).then_inc(W.free_sem(step), 1)
                    elif kind == "proj" and l == 1:
                        i = "qk".index(step[2])
                        act.wait_ge(*W.filled(b, step))
                        nc.scalar.activation(full[step[2]][:], W.bank(step)[:], ACT.Identity,
                                             bias=(bq_s, bk_s)[i][:, 0:1]).then_inc(W.free_sem(step), 1)
                    elif kind == "gate":
                        for i, n in enumerate("qk"):
                            act.wait_ge(*(full_done(b, i + 1) if l == 0 else W.emptied(b, ("proj", 1, n))))
                            nc.scalar.copy(parts[n][:, 0, :], full[n][:]).then_inc(hi_done[l].sem, 1)
                        for i, n in enumerate("qk"):
                            act.wait_ge(*rest_done[l](b, i + 1))
                            nc.scalar.copy(parts[n][:, 1, :], rest[n][:]).then_inc(mid_done[l].sem, 1)
                    elif kind == "v":
                        act.wait_ge(pool_consts.sem, 2)
                        if l == 0:
                            act.wait_ge(*W.filled(b, step))
                            nc.scalar.copy(v_ext[0][:, :, :, 0:DK], W.bank(step)[:].rearrange("p (k h d) -> p k h d", k=NBLK, h=HEADS))\
                              .then_inc(W.free_sem(step), 1)
                        if l == 1:
                            act.wait_ge(*gate_step[1](b, 2))
                            nc.scalar.activation(lg["exp"][:], lg["shift"][:], ACT.Exp).then_inc(gate_exp.sem, 1)
                    elif kind == "ohT":
                        rows = ohT[l].shape[0]
                        act.wait_ge(*W.filled(b, step))
                        nc.scalar.copy(ohT[l][:], W.bank(step)[:].bitcast(BF16)[0:rows, 0:SEQ]).then_inc(W.free_sem(step), 1)
                    elif kind == "h":
                        e, f = step[2:]
                        n = e * NF + f
                        act.wait_ge(*W.filled(b, step))
                        if n >= 4:
                            act.wait_ge(*hid_used(b, n - 3))
                        nc.scalar.activation(hid[n % 4][:], W.bank(step)[:], ACT.Relu).then_inc(W.free_sem(step), 1)
                    elif kind == "mT":
                        p = step[2]
                        act.wait_ge(*W.filled(b, step))
                        if p >= 2:
                            act.wait_ge(*mrow_in[l][p % 2](b, 32 * (p // 2)))
                        nc.scalar.copy(neg_row[p % 2][:], W.bank(step)[:].bitcast(BF16)[0:24, 0:P])\
                          .then_inc(W.free_sem(step), 1)
                    elif kind == "st":
                        p, j, kb = step[2:]
                        g, m, n = p // 2, 2 * (p % 2) + j, q0(l, kb)
                        if g >= 2 and m == 0 and kb == 0:
                            act.wait_ge(*pv_done[l](b, g - 1))
                        act.wait_ge(*T.filled(b, step))
                        nc.scalar.activation(probs[g % 2][:, m, kb, n:SEQ], T.bank(step)[:, n:SEQ], ACT.Exp,
                                             scale=INV_SQRT_DK).then_inc(T.free_sem(step), 1)
                    elif kind == "pv" and step[3] == NBLK - 1:
                        g = step[2]
                        act.wait_ge(*pv_done[l](b, g + 1))
                        if g >= 2:
                            act.wait_ge(*o_moved[l][g % 2](b, 16 * 8 * (g // 2)))
                        nc.scalar.copy(o_quad[g % 2][:], o_ps[:]).then_inc(o_out[l].sem, 1)
                    elif kind == "silu":
                        if l == 0:
                            act.wait_ge(*silu_sum(b))
                            nc.scalar.activation(y_sig[:], y_s[:], ACT.Exp, scale=-1.0).then_inc(silu_exp[0].sem, 1)
                        else:
                            act.wait_ge(*hid_used(b, E * NF))
                            nc.scalar.activation(y_sig[:], y_ps[:], ACT.Exp, scale=-1.0).then_inc(silu_exp[1].sem, 1)

        @block.vector
        def _(dve):
            dve.sem_inc(out_stored.sem, 16)
            for ring in (W, S, T):
                for i in range(2):
                    dve.sem_inc(ring.free[i].sem, 1)
            dve.wait_ge(consts_in.sem, N_LOADS)
            for dst, src in ((identb_s[:], ident_s[:]), (causalb_s[:], causal_s), (selectb_s[:], select_s)):
                dve.tensor_copy(dst, src).then_inc(consts_cast.sem, 1)
            dve.tensor_copy(keyrowb_s, keyrow_s.unsqueeze(1).to_broadcast([9, PAIRS, SEQ])).then_inc(consts_cast.sem, 1)
            dve.memset(neg_half[:], -0.5).then_inc(consts_cast.sem, 1)
            dve.tensor_scalar(slope_s[:, 1:2], slope_s[:, 0:1], float(DK) ** 0.5, None, ALU.mult).then_inc(slope_step.sem, 1)
            dve.wait_ge(slope_step.sem, 1)
            dve.tensor_copy(slope3_s[:, 0:1], slope_s[:, 1:2]).then_inc(slope_step.sem, 1)
            dve.wait_ge(slope_step.sem, 2)
            dve.tensor_tensor(slope_s[:, 2:3], slope_s[:, 1:2], slope3_s[:, 0:1], ALU.subtract).then_inc(slope_step.sem, 1)
            dve.wait_ge(slope_step.sem, 3)
            dve.tensor_copy(slope3_s[:, 1:2], slope_s[:, 2:3]).then_inc(slope_step.sem, 1)
            dve.wait_ge(slope_step.sem, 4)
            dve.tensor_tensor(slope3_s[:, 2:3], slope_s[:, 2:3], slope3_s[:, 1:2], ALU.subtract).then_inc(slope_step.sem, 1)
            dve.wait_ge(slope_step.sem, 5)
            dve.tensor_copy(sloperow_s, slope3_s[:].unsqueeze(2).to_broadcast([HEADS, 3, SEQ])).then_inc(slope_step.sem, 1)

            def over_experts(t):
                return t[:].unsqueeze(2).to_broadcast([P, NBLK, E])

            with dve.Fori(0, BATCH) as batch:
                b = Turn(dve, batch)
                def normalise(l):
                    if l == 0:
                        dve.wait_ge(*x_loaded(b, 16))
                    else:
                        dve.wait_ge(*W.emptied(b, ("xT", 0)))
                    for k in range(NBLK):
                        dve.bn_stats(ln_stat[l][:, k, :], x_s[l][:, k, :]).then_inc(stat_done[l].sem, 1)
                    for k in range(NBLK):
                        stats = stat_done[l](b, k + 1)
                        dve.wait_ge(consts_in.sem, N_LOADS)
                        dve.wait_ge(*stats)
                        dve.bn_aggr(ln_mv[l][:, k, :], ln_stat[l][:, k, :]).then_inc(aggr_done[l].sem, 1)
                    dve.wait_ge(*aggr_done[l](b, NBLK))
                    dve.tensor_scalar(ln_var[l][:], ln_mv[l][:, :, 1], EPS, None, ALU.add).then_inc(var_done[l].sem, 1)
                    dve.wait_ge(*rstd_done[l](b))
                    for k in range(NBLK):
                        ins = dve.tensor_scalar(xn[:, k, :], x_s[l][:, k, :], ln_mv[l][:, k, 0:1],
                                                ln_rstd[l][:, k:k + 1], ALU.subtract, ALU.mult)
                    ins.then_inc(xn_done[l].sem, 1)

                def gate_chain(l):
                    count = [0]

                    def link(ins):
                        count[0] += 1
                        ins.then_inc(gate_step[l].sem, 1)
                        dve.wait_ge(*gate_step[l](b, count[0]))

                    def first_max(src, mx, vmx, onehot):
                        link(dve.tensor_reduce(mx[:], src[:], AX.X, ALU.max))
                        link(dve.tensor_tensor(lg["eq"][:], src[:], over_experts(mx), ALU.is_equal))
                        link(dve.tensor_tensor(lg["val"][:], lg["eq"][:], rank_s[:], ALU.mult))
                        link(dve.tensor_reduce(vmx[:], lg["val"][:], AX.X, ALU.max))
                        link(dve.tensor_tensor(onehot[:], lg["val"][:], over_experts(vmx), ALU.is_equal))

                    dve.tensor_copy(lg["logit"][:], W.bank(("gate", l))[:, 0:NBLK * E].rearrange("p (k e) -> p k e", e=E))\
                       .then_inc(W.free_sem(("gate", l)), 1)
                    dve.wait_ge(*W.emptied(b, ("gate", l)))
                    if l == 0:
                        first_max(lg["logit"], lgs["max"], lgs["vmax"], onehot_b)
                    else:
                        link(dve.tensor_reduce(lgs["max"][:], lg["logit"][:], AX.X, ALU.max))
                        link(dve.tensor_tensor(lg["shift"][:], lg["logit"][:], over_experts(lgs["max"]), ALU.subtract))
                        dve.wait_ge(*gate_exp(b))
                        link(dve.tensor_reduce(lgs["sum"][:], lg["exp"][:], AX.X, ALU.add))
                        link(dve.reciprocal(lgs["rsum"][:], lgs["sum"][:]))
                        link(dve.tensor_tensor(lg["prob"][:], lg["exp"][:], over_experts(lgs["rsum"]), ALU.mult))
                        first_max(lg["prob"], lgs["max"], lgs["vmax"], lg["oh1"])
                        link(dve.scalar_tensor_tensor(out=lg["prob2"][:], in0=lg["oh1"][:], scalar=-2.0, in1=lg["prob"][:],
                                                      op0=ALU.mult, op1=ALU.add))
                        first_max(lg["prob2"], lgs["max2"], lgs["vmax2"], lg["oh2"])
                        link(dve.tensor_tensor(lg["both"][:], lg["oh1"][:], lg["oh2"][:], ALU.add))
                        link(dve.tensor_tensor(lg["prob2"][:], lg["prob"][:], lg["both"][:], ALU.mult))
                        link(dve.tensor_reduce(lgs["csum"][:], lg["prob2"][:], AX.X, ALU.add))
                        link(dve.reciprocal(lgs["rcsum"][:], lgs["csum"][:]))
                        link(dve.tensor_tensor(lg["comb"][:], lg["prob2"][:], over_experts(lgs["rcsum"]), ALU.mult))
                        link(dve.tensor_copy(comb3_b[:, :, 0, :], lg["comb"][:]))
                        link(dve.tensor_tensor(lg["rem"][:], lg["comb"][:], comb3_b[:, :, 0, :], ALU.subtract))
                        link(dve.tensor_copy(comb3_b[:, :, 1, :], lg["rem"][:]))
                        link(dve.tensor_tensor(comb3_b[:, :, 2, :], lg["rem"][:], comb3_b[:, :, 1, :], ALU.subtract))
                    assert count[0] == GATE_OPS[l], count[0]

                normalise(0)
                for step in STEPS:
                    kind, l = step[0], step[1]
                    if kind == "proj" and l == 0:
                        i = ("q", "qr", "k", "kr").index(step[2])
                        name, rotated = step[2][0], i % 2
                        dve.wait_ge(*W.filled(b, step))
                        dve.tensor_tensor((rope_b if rotated else rope_a)[name][:], W.bank(step)[:],
                                          (sin_s if rotated else cos_s)[:], ALU.mult).then_inc(W.free_sem(step), 1)
                        if rotated:
                            dve.wait_ge(*W.emptied(b, ("proj", 0, name)))
                            dve.wait_ge(*W.emptied(b, step))
                            dve.tensor_tensor(full[name][:], rope_a[name][:], rope_b[name][:], ALU.add)\
                               .then_inc(full_done.sem, 1)
                    elif kind == "gate":
                        for i, n in enumerate("qk"):
                            dve.wait_ge(*hi_done[l](b, i + 1))
                            dve.tensor_tensor(rest[n][:], full[n][:], parts[n][:, 0, :], ALU.subtract)\
                               .then_inc(rest_done[l].sem, 1)
                        for i, n in enumerate("qk"):
                            dve.wait_ge(*mid_done[l](b, i + 1))
                            dve.tensor_tensor(parts[n][:, 2, :], rest[n][:], parts[n][:, 1, :], ALU.subtract)\
                               .then_inc(lo_done[l].sem, 1)
                        dve.wait_ge(*W.filled(b, step))
                        gate_chain(l)
                    elif kind == "v" and l == 1:
                        dve.wait_ge(pool_consts.sem, 2)
                        dve.wait_ge(*W.filled(b, step))
                        dve.tensor_tensor(v_ext[1][:, :, :, 0:DK], W.bank(step)[:].rearrange("p (k h d) -> p k h d", k=NBLK, h=HEADS),
                                          bv_s[:].rearrange("p (o h d) -> p o h d", o=1, h=HEADS).to_broadcast([P, NBLK, HEADS, DK]),
                                          ALU.add).then_inc(W.free_sem(step), 1)
                    elif kind == "bc":
                        e = step[2]
                        dve.wait_ge(*W.filled(b, step))
                        if e >= 2:
                            dve.wait_ge(*(xe_used(b, e - 1) if l == 0 else W.filled(b, ("h", 1, e - 2, NF - 1))))
                        dve.tensor_tensor(x_e[e % 2][:], xnT[l][:], W.bank(step)[:], ALU.mult).then_inc(W.free_sem(step), 1)
                    elif kind == "s":
                        p, j, qb = step[2:]
                        if p >= 2 and j == 0 and qb == 0:
                            dve.wait_ge(*neg_step[l](b, 4 * (p - 1)))
                        dve.wait_ge(*S.filled(b, step))
                        ins = dve.tensor_reduce(neg_max[p % 2][:, j, qb:qb + 1], S.bank(step)[:, 0:w0(l, qb)], AX.X, ALU.max,
                                                negate=True)
                        ins.then_inc(S.free_sem(step), 1)
                    elif kind == "silu":
                        if l == 0:
                            dve.wait_ge(*xe_used(b, E))
                            dve.tensor_tensor(y_s[:], y_ps[:], xnT[0][:], ALU.add).then_inc(silu_sum.sem, 1)
                        dve.wait_ge(*silu_exp[l](b))
                        dve.tensor_scalar(y_sig[:], y_sig[:], 1.0, None, ALU.add).then_inc(silu_step[l].sem, 1)
                        dve.wait_ge(*silu_step[l](b, 1))
                        dve.reciprocal(y_sig[:], y_sig[:]).then_inc(silu_step[l].sem, 1)
                        dve.wait_ge(*silu_step[l](b, 2))
                        dve.tensor_tensor(g_s[:], (y_s if l == 0 else y_ps)[:], y_sig[:], ALU.mult).then_inc(silu_step[l].sem, 1)
                        for i in range(2):
                            dve.wait_ge(*o_moved[l][i](b, 16 * 8 * GROUPS // 2))
                        dve.reciprocal(o_den[:], o_den[:]).then_inc(norm_step[l].sem, 1)
                        dve.wait_ge(*norm_step[l](b, 1))
                        dve.tensor_tensor(o_heads[:], o_heads[:], o_den[:], ALU.mult).then_inc(norm_step[l].sem, 1)
                    elif kind == "wo":
                        dve.wait_ge(*W.filled(b, step))
                        dve.wait_ge(*silu_step[l](b, 3))
                        if l == 0:
                            dve.tensor_tensor(g_s[:], W.bank(step)[:], g_s[:], ALU.mult).then_inc(W.free_sem(step), 1)
                        else:
                            dve.scalar_tensor_tensor(out=g_s[:], in0=W.bank(step)[:], scalar=bo_s[:, 0:1], in1=g_s[:],
                                                     op0=ALU.add, op1=ALU.mult).then_inc(W.free_sem(step), 1)
                    elif kind == "xT":
                        dve.wait_ge(*W.filled(b, step))
                        dst = x_s[1] if l == 0 else x_out
                        if l == 1:
                            dve.wait_ge(*out_stored(b, 0))
                        dve.tensor_tensor(dst[:], W.bank(step)[:].rearrange("p (k d) -> p k d", k=NBLK), x_s[l][:], ALU.add)\
                           .then_inc(W.free_sem(step), 1)
                        if l == 0:
                            normalise(1)

        @block.gpsimd
        def _(pool):
            for l in LAYERS:
                nc.gpsimd.memset(v_ext[l][:], 1.0).then_inc(pool_consts.sem, 1)
            pool.wait_ge(consts_cast.sem, 5)
            with pool.Fori(0, BATCH) as batch:
                b = Turn(pool, batch)
                def rstd(l):
                    pool.wait_ge(*var_done[l](b))
                    nc.gpsimd.tensor_tensor(ln_rstd[l][:], ln_var[l][:], neg_half[:], ALU.pow).then_inc(rstd_done[l].sem, 1)

                rstd(0)
                for step in STEPS:
                    kind, l = step[0], step[1]
                    if kind == "mT":
                        p = step[2]
                        i, k = p % 2, 4 * p
                        if p >= 2:
                            pool.wait_ge(*W.filled(b, ("mT", l, p - 2)))
                        maxima = S.emptied(b, ("s", l, p, 1, NBLK - 1))
                        pool.wait_ge(consts_cast.sem, 5)
                        pool.wait_ge(*maxima)
                        nc.gpsimd.tensor_copy(neg3[i][:, :, 0, :], neg_max[i][:]).then_inc(neg_step[l].sem, 1)
                        pool.wait_ge(*neg_step[l](b, k + 1))
                        nc.gpsimd.tensor_tensor(neg_rest[i][:], neg_max[i][:], neg3[i][:, :, 0, :], ALU.subtract)\
                          .then_inc(neg_step[l].sem, 1)
                        rests = neg_step[l](b, k + 2)
                        pool.wait_ge(consts_cast.sem, 5)
                        pool.wait_ge(*rests)
                        nc.gpsimd.tensor_copy(neg3[i][:, :, 1, :], neg_rest[i][:]).then_inc(neg_step[l].sem, 1)
                        pool.wait_ge(*neg_step[l](b, k + 3))
                        nc.gpsimd.tensor_tensor(neg3[i][:, :, 2, :], neg_rest[i][:], neg3[i][:, :, 1, :], ALU.subtract)\
                          .then_inc(neg_step[l].sem, 1)
                    elif kind == "st" and l == 0:
                        p, j, kb = step[2:]
                        g, m, n = p // 2, 2 * (p % 2) + j, P * kb
                        exps = T.emptied(b, step)
                        pool.wait_ge(consts_cast.sem, 5)
                        pool.wait_ge(*exps)
                        v = probs[g % 2][:, m, kb, n:n + P]
                        nc.gpsimd.affine_select(out=v, in_=v, compare_op=ALU.is_ge, fill=0.0, base=0, pattern=[[1, P]],
                                                channel_multiplier=-1).then_inc(mask_done.sem, 1)
                    elif kind == "xT" and l == 0:
                        rstd(1)


_ORDER = ["x", "wq0", "wq0r", "wk0", "wk0r", "wv0", "wo0", "gate0", "expert0", "wq1", "wk1", "wv1", "wo1", "gate1",
          "w1", "w2", "bq1", "bk1", "bv1", "bo1", "slopes", "cos_t", "sin_t", "ident", "causal", "rank", "select",
          "key_rows"]


def kernel(**inputs):
    import numpy as np
    import concourse.bacc as bacc
    from concourse.bass_utils import run_bass_kernel_spmd as run

    a = {k: np.asarray(v) for k, v in inputs.items()}

    def shaped(v):
        return np.ascontiguousarray(v)

    qk = np.array([(2 * p + j) * DK + d for j in range(2) for d in range(DK) for p in range(PAIRS)])
    swap = np.array([(2 * p + j) * DK + (d ^ 1) for j in range(2) for d in range(DK) for p in range(PAIRS)])
    oo = np.array([(4 * g + m) * DK + d for m in range(4) for g in range(GROUPS) for d in range(DK)])
    ins = {"x": shaped(a["L0_attn_x"].reshape(BATCH, NBLK, P, D).transpose(0, 2, 1, 3))}
    for l in LAYERS:
        t = f"L{l}_attn_"
        ins[f"wq{l}"] = shaped(a[t + "Wq"][qk].T)
        ins[f"wk{l}"] = shaped(a[t + "Wk"][qk].T)
        ins[f"wv{l}"] = shaped(a[t + "Wv"].T)
        ins[f"wo{l}"] = shaped(a[t + "Wo"].T[oo])
    ins["wq0r"] = shaped(a["L0_attn_Wq"][swap].T)
    ins["wk0r"] = shaped(a["L0_attn_Wk"][swap].T)
    ins["gate0"] = shaped(a["L0_ffn_gate_w"].T)
    ins["gate1"] = shaped(a["L1_ffn_Wg"])
    ins["expert0"] = shaped(a["L0_ffn_expert_w"].transpose(2, 0, 1))
    ins["w1"] = shaped(a["L1_ffn_W1"].transpose(1, 0, 2))
    ins["w2"] = shaped(a["L1_ffn_W2"].reshape(E, NF, P, D).transpose(2, 0, 1, 3))
    ins["bq1"] = shaped(a["L1_attn_bq"][qk][:, None])
    ins["bk1"] = shaped(a["L1_attn_bk"][qk][:, None])
    ins["bv1"] = shaped(np.broadcast_to(a["L1_attn_bv"][None, :], (P, D)))
    ins["bo1"] = shaped(a["L1_attn_bo"][:, None])
    ins["slopes"] = shaped(a["L1_attn_slopes"].reshape(PAIRS, 2).T.reshape(HEADS, 1))

    half = DK // 2
    inv_freq = np.float32(10000.0) ** (-np.arange(half, dtype=np.float32) * np.float32(2.0) / np.float32(DK))
    angles = np.arange(SEQ, dtype=np.float32)[None, :] * inv_freq.astype(np.float32)[:, None]
    d_of = np.array([d for j in range(2) for d in range(DK) for p in range(PAIRS)])
    sign = np.where(d_of % 2 == 0, -1.0, 1.0).astype(np.float32)[:, None]
    ins["cos_t"] = shaped(np.cos(angles.astype(np.float64)).astype(np.float32)[d_of // 2])
    ins["sin_t"] = shaped(np.sin(angles.astype(np.float64)).astype(np.float32)[d_of // 2] * sign)
    ins["ident"] = np.eye(P, dtype=np.float32)
    r = np.arange(P)
    ins["causal"] = np.where(r[None, :] > r[:, None], np.float32(MASKED), np.float32(0))
    ins["rank"] = shaped(np.broadcast_to((E - np.arange(E)).astype(np.float32), (P, NBLK, E)))
    sel = np.zeros((3 * E, E, P), np.float32)
    for e in range(E):
        sel[e::E, e, :] = 1.0
    ins["select"] = sel
    dist = np.arange(SEQ) - (SEQ - 1)
    far = -(-dist // P) * P
    far = (dist // P) * P
    rows = [far] * 3 + [dist - far] * 3 + [np.ones(SEQ)] * 3
    ins["key_rows"] = np.stack(rows).astype(np.float32)

    nc = bacc.Bacc("TRN2", target_bir_lowering=False, num_devices=1)
    args = [nc.dram_tensor(f"in_{n}", ins[n].shape, F32, kind="ExternalInput").ap() for n in _ORDER]
    out = nc.dram_tensor("out", (BATCH, P, NBLK, D), F32, kind="ExternalOutput").ap()
    two_layer_kernel(nc, *args, out)
    r = run(nc, [{f"in_{n}": ins[n] for n in _ORDER}], core_ids=[0])
    y = r.results[0]["out"]
    return np.ascontiguousarray(y.transpose(0, 2, 1, 3).reshape(BATCH, SEQ, D))
```

```python
from contextlib import ExitStack, contextmanager

import concourse.bass as bass
from concourse import mybir

F32 = mybir.dt.float32
BF16 = mybir.dt.bfloat16
ALU = mybir.AluOpType
ACT = mybir.ActivationFunctionType
AX = mybir.AxisListType

P = 128
BATCH, SEQ, D = 8, 512, 128
HEADS, DK = 16, 8
PAIRS, GROUPS = HEADS // 2, HEADS // 4
NBLK = SEQ // P
E = 8
F = 256
NF = F // P
LAYERS = (0, 1)
EPS = 1e-5
INV_SQRT_DK = 1.0 / float(DK) ** 0.5
MASKED = -1e30
TERMS = [(0, 0), (0, 1), (0, 2), (1, 0), (1, 1), (2, 0)]
BIAS_ROW = 2 * DK * len(TERMS)
MAX_ROW = P - 3
VW = 32

NEXT, THIS, LAST = "next", "this", "last"
FRONT = ("ln", "xnT", "proj", "hi", "mid", "gate", "gexp", "gate2", "v", "ohT")
EXPERT = ("bc", "y0", "h", "y1", "silu")


def lag(step):
    kind, l = step[0], step[1]
    if l == 0:
        return -1 if kind in FRONT + EXPERT + ("ext",) else 0
    return 0 if kind in FRONT else 1


def spread(lanes):
    keyed = [((i + 0.5) / len(lane), n, i, s) for n, lane in enumerate(lanes) for i, s in enumerate(lane) if s]
    return [s for *_, s in sorted(keyed, key=lambda t: t[:3])]


def expert_steps(l):
    if l == 0:
        out = [("bc", 0, 0)]
        for e in range(E):
            out += ([("bc", 0, e + 1)] if e + 1 < E else []) + [("y0", 0, e)]
        return out
    out = [("bc", 1, 0)]
    for e in range(E):
        out += [("h", 1, e, f) for f in range(NF)] + ([("bc", 1, e + 1)] if e + 1 < E else [])
        out += [("y1", 1, e, f) for f in range(NF)]
    return out


def schedule(parts):
    score, turn, quad, fill = ([[] for _ in range(22)] for _ in range(4))
    for l, part, t0 in ((0, THIS, 0), (1, LAST, 8)):
        if part not in parts:
            continue
        for p in range(PAIRS):
            score[t0 + p] += [("s", l, p, j, qb) for j in range(2) for qb in range(NBLK)]
        for g in range(GROUPS):
            t = t0 + 2 * g
            st = [[("st", l, g, m, kb) for m in range(4)] for kb in range(NBLK)]
            pv = [[("pv", l, g, kb)] for kb in range(NBLK)]
            turn[t + 2] += [("mT", l, g), None, None]
            quad[t + 3] += st[0] + st[1] + pv[0]
            quad[t + 4] += st[2] + pv[1] + st[3] + pv[2]
            quad[t + 5] += pv[3]
    if LAST in parts:
        steps = expert_steps(1)
        for n, s in enumerate(steps):
            fill[n * 12 // len(steps)].append(s)
        for t in range(len(TERMS)):
            fill[t + 1].append(("ext", 1, t))
        fill[12] += [("silu", 1)]
    if THIS in parts:
        fill[10] += [("rcp", 0, c) for c in range(2)]
        fill[11] += [("rcp", 0, c) for c in range(2, NBLK)] + [("nrm", 0)]
        fill[12] += [("wo", 0), ("xT", 0)]
    if NEXT in parts:
        fill[13] += [("ln", 0), ("xnT", 0)]
        fill[14] += [("proj", 0, n) for n in ("q", "qr", "k", "kr")]
        fill[15] += [("gate", 0), ("hi", 0, "q"), ("v", 0), ("hi", 0, "k")]
        fill[16] += [("mid", 0, "q"), ("ohT", 0), ("mid", 0, "k")]
    if THIS in parts:
        fill[14] += [("ln", 1)]
        fill[15] += [("xnT", 1), ("gate", 1)]
        fill[16] += [("gexp", 1), ("gate2", 1)]
        fill[17] += [("ohT", 1)]
    if NEXT in parts:
        for t in range(len(TERMS)):
            fill[16 + (t + 1) // 2].append(("ext", 0, t))
        steps = expert_steps(0)
        for n, s in enumerate(steps):
            fill[17 + n * 4 // len(steps)].append(s)
    if THIS in parts:
        fill[18] += [("proj", 1, "q"), ("proj", 1, "k")]
        fill[20] += [("hi", 1, "q"), ("hi", 1, "k"), ("v", 1)]
        fill[21] += [("mid", 1, "q"), ("mid", 1, "k")]
    if LAST in parts:
        fill[20] += [("rcp", 1, c) for c in range(NBLK)] + [("nrm", 1)]
    if NEXT in parts:
        fill[21] += [("silu", 0)]
    if LAST in parts:
        fill[21] += [("wo", 1), ("xT", 1)]
    return [s for t in range(22) for s in spread((score[t], turn[t], quad[t], fill[t]))]


W_KINDS = ("xnT", "proj", "gate", "v", "ohT", "bc", "h", "mT", "wo", "xT")


class Segment:

    def __init__(self, first, end, parts, before):
        self.first, self.end, self.parts = first, end, parts
        self.steps = schedule(parts)
        self.uses, self.offset = {}, dict(before)
        for ring, kinds in (("work", W_KINDS), ("score", ("s",)), ("scoreT", ("st",))):
            self.uses[ring] = {s: n for n, s in enumerate(s for s in self.steps if s[0] in kinds)}
            before[ring] += len(self.uses[ring]) * (end - first)
        assert end - first == 1 or all(len(u) % 2 == 0 for u in self.uses.values())


def segments():
    before = {"work": 0, "score": 0, "scoreT": 0}
    return [Segment(-1, 0, (NEXT,), before), Segment(0, 1, (NEXT, THIS), before),
            Segment(1, BATCH - 1, (NEXT, THIS, LAST), before), Segment(BATCH - 1, BATCH, (THIS, LAST), before),
            Segment(BATCH, BATCH + 1, (LAST,), before)]


class Turn:

    def __init__(self, eng, seg, i, rises, rings):
        self.eng, self.seg, self.i, self.bases, self.waits = eng, seg, i, {}, 0
        self.looped = seg.end - seg.first > 1
        if self.looped:
            self.scratch = [eng.alloc_register(f"wait_value{n}") for n in range(8)]
            for per in sorted(set(rises) | {len(uses) // 2 for ring, uses in seg.uses.items() if ring in rings}):
                self.bases[per] = eng.alloc_register(f"iteration_times_{per}")
                eng.reg_mul(self.bases[per], i, per)

    def value(self, per, const):
        if not self.looped:
            assert self.i * per + const > 0
            return self.i * per + const
        assert self.seg.first * per + const > 0
        if const == 0:
            return self.bases[per]
        reg = self.scratch[self.waits % len(self.scratch)]
        self.waits += 1
        self.eng.reg_add(reg, self.bases[per], const)
        return reg


@contextmanager
def iterations(eng, seg, rises, rings=("work", "score", "scoreT")):
    if seg.end - seg.first > 1:
        with eng.Fori(seg.first, seg.end) as i:
            yield Turn(eng, seg, i, rises, rings)
    else:
        yield Turn(eng, seg, seg.first, (), ())


class Signal:

    def __init__(self, ctx, nc, name, per=1, credit=0):
        self.sem = ctx.enter_context(nc.semaphore(name))
        self.per, self.credit = per, credit

    def __call__(self, turn, lag, k=1):
        return self.sem, turn.value(self.per, self.credit + k - lag * self.per)


class Ring:

    def __init__(self, ctx, nc, name):
        self.name = name
        self.banks = [ctx.enter_context(nc.psum_tensor(f"{name}{i}", [P, SEQ], F32)) for i in range(2)]
        self.full = [ctx.enter_context(nc.semaphore(f"{name}_full{i}")) for i in range(2)]
        self.free = [ctx.enter_context(nc.semaphore(f"{name}_free{i}")) for i in range(2)]

    def place(self, turn, step):
        return turn.seg.offset[self.name] + turn.seg.uses[self.name][step]

    def count(self, turn, step, extra):
        per = len(turn.seg.uses[self.name]) // 2 if turn.looped else 0
        return turn.value(per, self.place(turn, step) // 2 + 1 + extra - per * turn.seg.first)

    def bank(self, turn, step):
        return self.banks[self.place(turn, step) % 2]

    def filled(self, turn, step):
        return self.full[self.place(turn, step) % 2], self.count(turn, step, 0)

    def freed(self, turn, step):
        return self.free[self.place(turn, step) % 2], self.count(turn, step, 0)

    def emptied(self, turn, step):
        return self.free[self.place(turn, step) % 2], self.count(turn, step, 1)

    def full_sem(self, turn, step):
        return self.full[self.place(turn, step) % 2]

    def free_sem(self, turn, step):
        return self.free[self.place(turn, step) % 2]


def two_layer_kernel(nc, x, wq0, wq0r, wk0, wk0r, wv0, wo0, gate0, expert0, wq1, wk1, wv1, wo1, gate1, w1, w2,
                     bq1, bk1, bv1, bo1, slopes, cos_t, sin_t, ident, causal, rank, select, key_rows, out):
    ctx = ExitStack()
    with ctx:
        def sb(name, shape, dt=F32):
            return ctx.enter_context(nc.sbuf_tensor(name, shape, dt))

        def sig(name, per=1, credit=0):
            return Signal(ctx, nc, name, per, credit)

        proj_w = {(0, "q"): sb("wq0_s", [P, D]), (0, "qr"): sb("wq0r_s", [P, D]), (0, "k"): sb("wk0_s", [P, D]),
                  (0, "kr"): sb("wk0r_s", [P, D]), (1, "q"): sb("wq1_s", [P, D]), (1, "k"): sb("wk1_s", [P, D])}
        wv_s = [sb("wv0_s", [P, D]), sb("wv1_s", [P, D])]
        wo_s = [sb("wo0_s", [P, D]), sb("wo1_s", [P, D])]
        gate_s = [sb("gate0_s", [P, E]), sb("gate1_s", [P, E])]
        expert_s = sb("expert_s", [P, E, D])
        w1_s = sb("w1_s", [P, E, F])
        w2_s = sb("w2_s", [P, E, NF, D])
        bq_s, bk_s, bo_s = sb("bq_s", [P, 1]), sb("bk_s", [P, 1]), sb("bo_s", [P, 1])
        bv_s = sb("bv_s", [P, D])
        cos_s, sin_s = sb("cos_s", [P, SEQ]), sb("sin_s", [P, SEQ])
        ident_s, identb_s = sb("ident_s", [P, P]), sb("identb_s", [P, P], BF16)
        causalb_s = sb("causalb_s", [P, P], BF16)
        rank_s = sb("rank_s", [P, NBLK, E])
        selectb_s = sb("selectb_s", [3 * E, E, P], BF16)
        slope_s, slope3_s = sb("slope_s", [HEADS, 4]), sb("slope3_s", [HEADS, 3], BF16)
        neg_half = sb("neg_half", [P, NBLK])

        x_in, x_mid, x_hold, x_out = (sb(n, [P, NBLK, D]) for n in ("x_in", "x_mid", "x_hold", "x_out"))
        ln_src = (x_in, x_mid)
        ln_stat = [sb(f"ln_stat{l}", [P, NBLK, 6]) for l in LAYERS]
        ln_mv = [sb(f"ln_mv{l}", [P, NBLK, 2]) for l in LAYERS]
        ln_var = [sb(f"ln_var{l}", [P, NBLK]) for l in LAYERS]
        ln_rstd = [sb(f"ln_rstd{l}", [P, NBLK]) for l in LAYERS]
        xn = sb("xn", [P, NBLK, D])
        xnT = [sb(f"xnT{l}", [P, SEQ]) for l in LAYERS]
        rope_a = {n: sb(f"rope_a_{n}", [P, SEQ]) for n in "qk"}
        rope_b = {n: sb(f"rope_b_{n}", [P, SEQ]) for n in "qk"}
        full = {n: sb(f"full_{n}", [P, SEQ]) for n in "qk"}
        rest = rope_a
        parts = {n: sb(f"parts_{n}", [P, 3, SEQ], BF16) for n in "qk"}
        k_ext = [sb(f"k_ext{l}", [P, PAIRS, SEQ], BF16) for l in LAYERS]
        q_ext = [[sb(f"q_ext{l}_{j}", [P, PAIRS, SEQ], BF16) for j in range(2)] for l in LAYERS]
        v_ext = [sb(f"v_ext{l}", [P, NBLK, HEADS, VW]) for l in LAYERS]
        neg_max = [sb(f"neg_max{i}", [P, 2, 2, NBLK]) for i in range(2)]
        neg_rest = [sb(f"neg_rest{i}", [P, 2, 2, NBLK]) for i in range(2)]
        neg3 = [sb(f"neg3_{i}", [P, 2, 3, 2, NBLK], BF16) for i in range(2)]
        NEG_ROWS = 3 * 2 * NBLK
        neg_row = [sb(f"neg_row{i}", [2 * NEG_ROWS, P], BF16) for i in range(2)]
        probs = sb("probs", [P, NBLK, 4, SEQ])
        stage = probs[:].rearrange("p k m n -> p (k m n)")
        select_s = stage[0:3 * E, 0:E * P].rearrange("p (e n) -> p e n", e=E)
        keyrow_s = stage[0:9, 1024:1536]
        keyrowb_s = stage[0:9, 1536:3584].bitcast(BF16).rearrange("p (h n) -> p h n", h=PAIRS)
        sloperow_s = stage[0:HEADS, 3584:4352].bitcast(BF16).rearrange("p (a n) -> p a n", a=3)
        causal_s = stage[:, 4352:4352 + P]
        o_quad = sb("o_quad", [P, GROUPS, SEQ])
        o_heads = [sb(f"o_heads{l}", [P, SEQ]) for l in LAYERS]
        o_den = [sb(f"o_den{l}", [P, SEQ]) for l in LAYERS]
        lg = {n: sb(f"g_{n}", [P, NBLK, E]) for n in
              ("logit", "eq", "val", "oh1", "oh2", "exp", "prob", "prob2", "both", "comb", "rem")}
        g_shift = sb("g_shift", [P, NBLK, E])
        lgs = {n: sb(f"gs_{n}", [P, NBLK]) for n in
               ("max", "vmax", "sum", "rsum", "max2", "vmax2", "csum", "rcsum")}
        onehot_b = sb("onehot_b", [P, NBLK, E], BF16)
        comb3_b = sb("comb3_b", [P, NBLK, 3, E], BF16)
        ohT = [sb("ohT0", [E, SEQ], BF16), sb("ohT1", [3 * E, SEQ], BF16)]
        x_e = [sb(f"x_e{i}", [P, SEQ]) for i in range(2)]
        hid = [sb(f"hid{i}", [P, SEQ]) for i in range(2)]
        y_s, y_sig = sb("y_s", [P, SEQ]), sb("y_sig", [P, SEQ])
        g_s = [sb(f"g_s{l}", [P, SEQ]) for l in LAYERS]

        W, S, T = Ring(ctx, nc, "work"), Ring(ctx, nc, "score"), Ring(ctx, nc, "scoreT")
        o_ps = ctx.enter_context(nc.psum_tensor("o_ps", [P, SEQ], F32))
        y_ps = ctx.enter_context(nc.psum_tensor("y_ps", [P, SEQ], F32))

        def per_layer(name, per=1):
            return [sig(f"{name}_{l}", per) for l in LAYERS]

        consts_in, consts_cast, slope_step, zeroed, ones_set, static_rows = (
            ctx.enter_context(nc.semaphore(n)) for n in
            ("consts_in", "consts_cast", "slope_step", "zeroed", "ones_set", "static_rows"))
        x_loaded = sig("x_loaded", 16)
        stat_done, aggr_done = per_layer("stat_done", NBLK), per_layer("aggr_done", NBLK)
        var_done, rstd_done, xn_done = per_layer("var_done"), per_layer("rstd_done"), per_layer("xn_done")
        full_done = sig("full_done", 2)
        hi_done, rest_done, mid_done, lo_done = (per_layer(n, 2) for n in ("hi_done", "rest_done", "mid_done", "lo_done"))
        EXT_DMAS = 3 * len(TERMS)
        ext_done = per_layer("ext_done", 16 * EXT_DMAS)
        GATE_OPS = (5, 25)
        gate_step = [sig(f"gate_step_{l}", GATE_OPS[l]) for l in LAYERS]
        gate_exp = sig("gate_exp")
        y_full = per_layer("y_full")
        neg_step = per_layer("neg_step", 4 * GROUPS)
        mrow_in = [[sig(f"mrow_in{l}_{i}", 32 * GROUPS // 2) for i in range(2)] for l in LAYERS]
        mask_done = sig("mask_done", GROUPS * NBLK)
        pv_done = per_layer("pv_done", GROUPS)
        o_out = per_layer("o_out", GROUPS)
        o_moved = per_layer("o_moved", 16 * 8)
        rcp_done, nrm_done = per_layer("rcp_done", NBLK), per_layer("nrm_done")
        y_read, tanh_done, sig_done, g_done = sig("y_read"), per_layer("tanh_done"), per_layer("sig_done"), per_layer("g_done")
        held = sig("held")
        out_stored = sig("out_stored", 16, credit=16)

        LOADS = [(proj_w[0, "q"], wq0), (proj_w[0, "qr"], wq0r), (proj_w[0, "k"], wk0), (proj_w[0, "kr"], wk0r),
                 (ident_s, ident), (gate_s[0], gate0), (wv_s[0], wv0), (cos_s, cos_t), (sin_s, sin_t), (rank_s, rank),
                 (proj_w[1, "q"], wq1), (proj_w[1, "k"], wk1), (wv_s[1], wv1), (wo_s[0], wo0),
                 (wo_s[1], wo1), (gate_s[1], gate1), (expert_s, expert0), (w1_s, w1),
                 (w2_s, w2), (bq_s, bq1), (bk_s, bk1), (bv_s, bv1), (bo_s, bo1)]
        LOADS = [(t[:], src) for t, src in LOADS] + [(causal_s, causal), (select_s, select), (keyrow_s, key_rows),
                                                     (slope_s[:, 0:1], slopes)]
        N_LOADS = 16 * len(LOADS)
        N_CASTS = 5
        N_ZERO = 6
        N_STATIC = 16 * (2 + 3 * 6)
        SEGMENTS = segments()

        def keys_of(l, qb):
            return P * (qb + 1) if l == 0 else SEQ

        def first_query(l, kb):
            return P * kb if l == 0 else 0

        block = ctx.enter_context(nc.Block())

        @block.sync
        def _(sp):
            sp.dma_start(x_in[:], x[0]).then_inc(x_loaded.sem, 16)
            for dst, src in LOADS:
                sp.dma_start(dst, src).then_inc(consts_in, 16)
            sp.wait_ge(zeroed, N_ZERO)
            sp.wait_ge(consts_cast, N_CASTS)
            sp.dma_start(k_ext[0][MAX_ROW:P], keyrowb_s[6:9]).then_inc(static_rows, 16)
            sp.dma_start(k_ext[1][MAX_ROW:P], keyrowb_s[6:9]).then_inc(static_rows, 16)
            sp.wait_ge(slope_step, 6)
            for n in range(6):
                sp.dma_start(k_ext[1][BIAS_ROW + n:BIAS_ROW + n + 1], keyrowb_s[n:n + 1]).then_inc(static_rows, 16)
                for j in range(2):
                    sp.dma_start(q_ext[1][j][BIAS_ROW + n:BIAS_ROW + n + 1], sloperow_s[PAIRS * j:PAIRS * (j + 1), n % 3, :])\
                      .then_inc(static_rows, 16)

            for seg in SEGMENTS:
                with iterations(sp, seg, (2, NBLK), ("work", "scoreT")) as t:
                    for step in seg.steps:
                        kind, l, g = step[0], step[1], lag(step)
                        if kind == "ext":
                            n = step[2]
                            waits = []
                            if n == 0:
                                waits.append(lo_done[l](t, g, 2))
                                if l == 0 and THIS in seg.parts:
                                    waits.append(T.filled(t, ("st", 0, GROUPS - 1, 3, NBLK - 1)))
                            for wait in waits:
                                sp.wait_ge(*wait)
                            qp, kp = TERMS[n]
                            row = 2 * DK * n
                            sp.dma_start(k_ext[l][row:row + 2 * DK], parts["k"][:, kp, :]).then_inc(ext_done[l].sem, 16)
                            for j in range(2):
                                sp.dma_start(q_ext[l][j][row + DK * j:row + DK * j + DK],
                                             parts["q"][64 * j:64 * j + 64, qp, :]).then_inc(ext_done[l].sem, 16)
                        elif kind == "mT":
                            grp = step[2]
                            sp.wait_ge(*W.emptied(t, step))
                            for j in range(2):
                                dst = q_ext[l][j][MAX_ROW:P, 2 * grp:2 * grp + 2, :].rearrange("r a (k n) -> r (a k) n", k=NBLK)
                                sp.dma_start(dst, neg_row[grp % 2][NEG_ROWS * j:NEG_ROWS * (j + 1), :])\
                                  .then_inc(mrow_in[l][grp % 2].sem, 16)
                        elif kind == "pv" and step[2:] == (GROUPS - 1, NBLK - 1):
                            sp.wait_ge(*o_out[l](t, g, GROUPS))
                            for m in range(4):
                                to = slice(32 * m, 32 * m + 32)
                                sp.dma_start(o_heads[l][to], o_quad[32 * m:32 * m + DK]).then_inc(o_moved[l].sem, 16)
                                sp.dma_start(o_den[l][to], o_quad[32 * m + DK:32 * m + 2 * DK]).then_inc(o_moved[l].sem, 16)
                        elif kind == "xT":
                            sum_done = W.emptied(t, step)
                            sp.wait_ge(zeroed, N_ZERO)
                            sp.wait_ge(*sum_done)
                            if l == 1:
                                sp.dma_start(out[t.i - 1], x_out[:]).then_inc(out_stored.sem, 16)
                            elif NEXT in seg.parts:
                                sp.dma_start(x_in[:], x[t.i + 1]).then_inc(x_loaded.sem, 16)
            sp.wait_ge(out_stored.sem, out_stored.credit + 16 * BATCH)

        @block.tensor
        def _(pe):
            pe.wait_ge(consts_in, N_LOADS)
            pe.wait_ge(consts_cast, N_CASTS)
            pe.wait_ge(static_rows, N_STATIC)
            pe.wait_ge(ones_set, 2)

            def steps(t):
                for step in t.seg.steps:
                    kind, l, g = step[0], step[1], lag(step)
                    if kind in W_KINDS:
                        bank = W.bank(t, step)
                        bank_b = bank[:].bitcast(BF16)
                        full_sem = W.full_sem(t, step)
                    if kind == "xnT":
                        pe.wait_ge(*xn_done[l](t, g))
                        pe.wait_ge(*W.freed(t, step))
                        for k in range(NBLK):
                            mm = pe.transpose(bank[:, P * k:P * k + P], xn[:, k, :], ident_s[:])
                        mm.then_inc(full_sem, 1)
                    elif kind == "proj":
                        pe.wait_ge(*W.emptied(t, ("xnT", l)))
                        pe.wait_ge(*W.freed(t, step))
                        pe.matmul(bank[:], proj_w[l, step[2]][:], xnT[l][:], start=True, stop=True).then_inc(full_sem, 1)
                    elif kind in ("gate", "v"):
                        rhs, n = (gate_s[l], E) if kind == "gate" else (wv_s[l], P)
                        pe.wait_ge(*W.emptied(t, ("xnT", l)))
                        pe.wait_ge(*W.freed(t, step))
                        for k in range(NBLK):
                            mm = pe.matmul(bank[:, n * k:n * k + n], xnT[l][:, P * k:P * k + P], rhs[:], start=True, stop=True)
                        mm.then_inc(full_sem, 1)
                    elif kind == "ohT":
                        pe.wait_ge(*gate_step[l](t, g, GATE_OPS[l]))
                        pe.wait_ge(*W.freed(t, step))
                        rows = ohT[l].shape[0]
                        for k in range(NBLK):
                            src = onehot_b[:, k, :] if l == 0 else comb3_b[:, k, :, :].rearrange("p a e -> p (a e)")
                            mm = pe.transpose(bank_b[0:rows, P * k:P * k + P], src, identb_s[:])
                        mm.then_inc(full_sem, 1)
                    elif kind == "bc":
                        e = step[2]
                        if l == 0:
                            pe.wait_ge(*W.emptied(t, ("ohT", 0)))
                        pe.wait_ge(*W.freed(t, step))
                        pe.matmul(bank[:], selectb_s[0:ohT[l].shape[0], e, :], ohT[l][:], start=True, stop=True)\
                          .then_inc(full_sem, 1)
                    elif kind == "y0":
                        e = step[2]
                        pe.wait_ge(*W.emptied(t, ("bc", 0, e)))
                        if e == 0 and LAST in t.seg.parts:
                            pe.wait_ge(*g_done[1](t, 1))
                        mm = pe.matmul(y_ps[:], expert_s[:, e, :], x_e[e % 2][:], start=e == 0, stop=e == E - 1)
                        if e == E - 1:
                            mm.then_inc(y_full[0].sem, 1)
                    elif kind == "h":
                        e, f = step[2:]
                        pe.wait_ge(*W.emptied(t, ("bc", 1, e)))
                        pe.wait_ge(*W.freed(t, step))
                        pe.matmul(bank[:], w1_s[:, e, P * f:P * f + P], x_e[e % 2][:], start=True, stop=True).then_inc(full_sem, 1)
                    elif kind == "y1":
                        e, f = step[2:]
                        pe.wait_ge(*W.emptied(t, ("h", 1, e, f)))
                        if e == 0 and f == 0 and THIS in t.seg.parts:
                            pe.wait_ge(*y_read(t, 0))
                        mm = pe.matmul(y_ps[:], w2_s[:, e, f, :], hid[f][:], start=e == 0 and f == 0, stop=e == E - 1 and f == NF - 1)
                        if e == E - 1 and f == NF - 1:
                            mm.then_inc(y_full[1].sem, 1)
                    elif kind == "s":
                        p, j, qb = step[2:]
                        if p == 0 and j == 0 and qb == 0:
                            pe.wait_ge(*ext_done[l](t, g, 16 * EXT_DMAS))
                        pe.wait_ge(*S.freed(t, step))
                        n, bank = keys_of(l, qb), S.bank(t, step)
                        mm = pe.matmul(bank[:, 0:n], q_ext[l][j][0:MAX_ROW, p, P * qb:P * qb + P],
                                       k_ext[l][0:MAX_ROW, p, 0:n], start=True, stop=l == 1)
                        if l == 0:
                            mm = pe.matmul(bank[:, P * qb:n], identb_s[:], causalb_s[:], start=False, stop=True)
                        mm.then_inc(S.full_sem(t, step), 1)
                    elif kind == "mT":
                        grp = step[2]
                        split, freed = neg_step[l](t, g, 4 * grp + 4), W.freed(t, step)
                        pe.wait_ge(consts_cast, N_CASTS)
                        pe.wait_ge(*split)
                        pe.wait_ge(*freed)
                        pe.transpose(bank_b[0:2 * NEG_ROWS, 0:P], neg3[grp % 2][:].rearrange("p j a b k -> p (j a b k)"), identb_s[:])\
                          .then_inc(full_sem, 1)
                    elif kind == "st":
                        grp, m, kb = step[2:]
                        p, j = 2 * grp + m // 2, m % 2
                        if m == 0 and kb == 0:
                            pe.wait_ge(*mrow_in[l][grp % 2](t, g, 32 * (grp // 2 + 1)))
                        pe.wait_ge(*T.freed(t, step))
                        n = first_query(l, kb)
                        pe.matmul(T.bank(t, step)[:, n:SEQ], k_ext[l][:, p, P * kb:P * kb + P], q_ext[l][j][:, p, n:SEQ],
                                  start=True, stop=True).then_inc(T.full_sem(t, step), 1)
                    elif kind == "pv":
                        grp, kb = step[2:]
                        if l == 0:
                            pe.wait_ge(*mask_done(t, g, NBLK * grp + kb + 1))
                        pe.wait_ge(*T.emptied(t, ("st", l, grp, 3, kb)))
                        if kb == 0 and grp > 0:
                            pe.wait_ge(*o_out[l](t, g, grp))
                        if kb == 0 and grp == 0 and l == 1 and THIS in t.seg.parts:
                            pe.wait_ge(*o_out[0](t, 0, GROUPS))
                        n = first_query(l, kb)
                        for m in range(4):
                            mm = pe.matmul(o_ps[32 * m:32 * m + VW, n:SEQ], v_ext[l][:, kb, 4 * grp + m, :],
                                           probs[:, kb, m, n:SEQ], start=kb == 0, stop=kb == NBLK - 1)
                        if kb == NBLK - 1:
                            mm.then_inc(pv_done[l].sem, 1)
                    elif kind == "wo":
                        pe.wait_ge(*nrm_done[l](t, g))
                        pe.wait_ge(*W.freed(t, step))
                        pe.matmul(bank[:], wo_s[l][:], o_heads[l][:], start=True, stop=True).then_inc(full_sem, 1)
                    elif kind == "xT":
                        pe.wait_ge(*W.emptied(t, ("wo", l)))
                        pe.wait_ge(*W.freed(t, step))
                        for k in range(NBLK):
                            mm = pe.transpose(bank[:, P * k:P * k + P], g_s[l][:, P * k:P * k + P], ident_s[:])
                        mm.then_inc(full_sem, 1)

            for seg in SEGMENTS:
                with iterations(pe, seg, (1, NBLK, GATE_OPS[0], GATE_OPS[1], 4 * GROUPS, 16 * GROUPS, 16 * EXT_DMAS)) as turn:
                    steps(turn)

        @block.scalar
        def _(act):
            act.wait_ge(consts_in, N_LOADS)
            act.wait_ge(consts_cast, N_CASTS)
            act.wait_ge(static_rows, N_STATIC)
            act.wait_ge(ones_set, 2)

            def steps(t):
                for step in t.seg.steps:
                    kind, l, g = step[0], step[1], lag(step)
                    if kind == "xnT":
                        act.wait_ge(*W.filled(t, step))
                        nc.scalar.copy(xnT[l][:], W.bank(t, step)[:]).then_inc(W.free_sem(t, step), 1)
                    elif kind == "proj" and l == 1:
                        bias = {"q": bq_s, "k": bk_s}[step[2]]
                        if step[2] == "q" and NEXT in t.seg.parts:
                            act.wait_ge(*rest_done[0](t, -1, 2))
                        act.wait_ge(*W.filled(t, step))
                        nc.scalar.activation(full[step[2]][:], W.bank(t, step)[:], ACT.Identity, bias=bias[:, 0:1])\
                          .then_inc(W.free_sem(t, step), 1)
                    elif kind == "hi":
                        i = "qk".index(step[2])
                        if i == 0 and l == 1 and NEXT in t.seg.parts:
                            act.wait_ge(*ext_done[0](t, -1, 16 * EXT_DMAS))
                        if i == 0 and l == 0 and LAST in t.seg.parts:
                            act.wait_ge(*ext_done[1](t, 1, 16 * EXT_DMAS))
                        act.wait_ge(*(full_done(t, g, i + 1) if l == 0 else W.emptied(t, ("proj", 1, step[2]))))
                        nc.scalar.copy(parts[step[2]][:, 0, :], full[step[2]][:]).then_inc(hi_done[l].sem, 1)
                    elif kind == "mid":
                        i = "qk".index(step[2])
                        act.wait_ge(*rest_done[l](t, g, i + 1))
                        nc.scalar.copy(parts[step[2]][:, 1, :], rest[step[2]][:]).then_inc(mid_done[l].sem, 1)
                    elif kind == "v" and l == 0:
                        act.wait_ge(*W.filled(t, step))
                        nc.scalar.copy(v_ext[0][:, :, :, 0:DK], W.bank(t, step)[:].rearrange("p (k h d) -> p k h d", k=NBLK, h=HEADS))\
                          .then_inc(W.free_sem(t, step), 1)
                    elif kind == "gexp":
                        act.wait_ge(*gate_step[1](t, g, 2))
                        nc.scalar.activation(lg["exp"][:], g_shift[:], ACT.Exp).then_inc(gate_exp.sem, 1)
                    elif kind == "ohT":
                        act.wait_ge(*W.filled(t, step))
                        nc.scalar.copy(ohT[l][:], W.bank(t, step)[:].bitcast(BF16)[0:ohT[l].shape[0], 0:SEQ])\
                          .then_inc(W.free_sem(t, step), 1)
                    elif kind == "h":
                        act.wait_ge(*W.filled(t, step))
                        nc.scalar.activation(hid[step[3]][:], W.bank(t, step)[:], ACT.Relu).then_inc(W.free_sem(t, step), 1)
                    elif kind == "mT":
                        grp = step[2]
                        act.wait_ge(*W.filled(t, step))
                        if grp >= 2:
                            act.wait_ge(*mrow_in[l][grp % 2](t, g, 32 * (grp // 2)))
                        nc.scalar.copy(neg_row[grp % 2][:], W.bank(t, step)[:].bitcast(BF16)[0:2 * NEG_ROWS, 0:P])\
                          .then_inc(W.free_sem(t, step), 1)
                    elif kind == "st":
                        grp, m, kb = step[2:]
                        n = first_query(l, kb)
                        act.wait_ge(*T.filled(t, step))
                        nc.scalar.activation(probs[:, kb, m, n:SEQ], T.bank(t, step)[:, n:SEQ], ACT.Exp,
                                             scale=INV_SQRT_DK).then_inc(T.free_sem(t, step), 1)
                    elif kind == "pv" and step[3] == NBLK - 1:
                        grp = step[2]
                        act.wait_ge(*pv_done[l](t, g, grp + 1))
                        if grp == 0 and l == 1 and THIS in t.seg.parts:
                            act.wait_ge(*o_moved[0](t, 0, 16 * 8))
                        nc.scalar.copy(o_quad[:, grp, :], o_ps[:]).then_inc(o_out[l].sem, 1)
                    elif kind == "silu":
                        if l == 0:
                            act.wait_ge(*y_read(t, g))
                        else:
                            act.wait_ge(*y_full[1](t, g))
                        nc.scalar.activation(y_sig[:], (y_s if l == 0 else y_ps)[:], ACT.Tanh, scale=0.5).then_inc(tanh_done[l].sem, 1)

            for seg in SEGMENTS:
                with iterations(act, seg, (1, 2, NBLK, GATE_OPS[1], 16 * GROUPS, 16 * 8, 16 * EXT_DMAS), ("work", "scoreT")) as turn:
                    steps(turn)

        @block.vector
        def _(dve):
            dve.sem_inc(out_stored.sem, 16)
            for ring in (W, S, T):
                for i in range(2):
                    dve.sem_inc(ring.free[i], 1)
            for tile in (k_ext[1], q_ext[1][0], q_ext[1][1]):
                dve.memset(tile[:].rearrange("p h n -> p (h n)").bitcast(F32), 0.0).then_inc(zeroed, 1)
            dve.wait_ge(consts_in, N_LOADS)
            dve.tensor_scalar(slope_s[:, 1:2], slope_s[:, 0:1], float(DK) ** 0.5, None, ALU.mult).then_inc(slope_step, 1)
            dve.wait_ge(slope_step, 1)
            dve.tensor_copy(slope3_s[:, 0:1], slope_s[:, 1:2]).then_inc(slope_step, 1)
            dve.wait_ge(slope_step, 2)
            dve.tensor_tensor(slope_s[:, 2:3], slope_s[:, 1:2], slope3_s[:, 0:1], ALU.subtract).then_inc(slope_step, 1)
            dve.wait_ge(slope_step, 3)
            dve.tensor_copy(slope3_s[:, 1:2], slope_s[:, 2:3]).then_inc(slope_step, 1)
            dve.wait_ge(slope_step, 4)
            dve.tensor_tensor(slope3_s[:, 2:3], slope_s[:, 2:3], slope3_s[:, 1:2], ALU.subtract).then_inc(slope_step, 1)
            dve.wait_ge(slope_step, 5)
            dve.tensor_copy(sloperow_s, slope3_s[:].unsqueeze(2).to_broadcast([HEADS, 3, SEQ])).then_inc(slope_step, 1)
            dve.tensor_copy(keyrowb_s, keyrow_s.unsqueeze(1).to_broadcast([9, PAIRS, SEQ])).then_inc(consts_cast, 1)
            for dst, src in ((identb_s[:], ident_s[:]), (causalb_s[:], causal_s), (selectb_s[:], select_s)):
                dve.tensor_copy(dst, src).then_inc(consts_cast, 1)
            dve.memset(neg_half[:], -0.5).then_inc(consts_cast, 1)

            def over_experts(t):
                return t[:].unsqueeze(2).to_broadcast([P, NBLK, E])

            def normalise(t, l, g):
                if l == 0:
                    dve.wait_ge(*x_loaded(t, g, 16))
                else:
                    dve.wait_ge(*W.emptied(t, ("xT", 0)))
                src = ln_src[l]
                for k in range(NBLK):
                    dve.bn_stats(ln_stat[l][:, k, :], src[:, k, :]).then_inc(stat_done[l].sem, 1)
                for k in range(NBLK):
                    stats = stat_done[l](t, g, k + 1)
                    dve.wait_ge(consts_in, N_LOADS)
                    dve.wait_ge(*stats)
                    dve.bn_aggr(ln_mv[l][:, k, :], ln_stat[l][:, k, :]).then_inc(aggr_done[l].sem, 1)
                dve.wait_ge(*aggr_done[l](t, g, NBLK))
                dve.tensor_scalar(ln_var[l][:], ln_mv[l][:, :, 1], EPS, None, ALU.add).then_inc(var_done[l].sem, 1)
                dve.wait_ge(*rstd_done[l](t, g))
                if l == 1 and NEXT in t.seg.parts:
                    dve.wait_ge(*W.filled(t, ("xnT", 0)))
                for k in range(NBLK):
                    ins = dve.tensor_scalar(xn[:, k, :], src[:, k, :], ln_mv[l][:, k, 0:1], ln_rstd[l][:, k:k + 1],
                                            ALU.subtract, ALU.mult)
                ins.then_inc(xn_done[l].sem, 1)

            def gate_chain(t, l, g, second):
                count = [2 if second else 0]

                def link(ins):
                    count[0] += 1
                    ins.then_inc(gate_step[l].sem, 1)
                    dve.wait_ge(*gate_step[l](t, g, count[0]))

                def first_max(src, mx, vmx, onehot):
                    link(dve.tensor_reduce(mx[:], src[:], AX.X, ALU.max))
                    link(dve.tensor_tensor(lg["eq"][:], src[:], over_experts(mx), ALU.is_equal))
                    link(dve.tensor_tensor(lg["val"][:], lg["eq"][:], rank_s[:], ALU.mult))
                    link(dve.tensor_reduce(vmx[:], lg["val"][:], AX.X, ALU.max))
                    link(dve.tensor_tensor(onehot[:], lg["val"][:], over_experts(vmx), ALU.is_equal))

                if not second:
                    step = ("gate", l)
                    dve.wait_ge(*W.filled(t, step))
                    dve.tensor_copy(lg["logit"][:], W.bank(t, step)[:, 0:NBLK * E].rearrange("p (k e) -> p k e", e=E))\
                       .then_inc(W.free_sem(t, step), 1)
                    dve.wait_ge(*W.emptied(t, step))
                if l == 0:
                    first_max(lg["logit"], lgs["max"], lgs["vmax"], onehot_b)
                elif not second:
                    link(dve.tensor_reduce(lgs["max"][:], lg["logit"][:], AX.X, ALU.max))
                    link(dve.tensor_tensor(g_shift[:], lg["logit"][:], over_experts(lgs["max"]), ALU.subtract))
                    return
                else:
                    dve.wait_ge(*gate_exp(t, g))
                    link(dve.tensor_reduce(lgs["sum"][:], lg["exp"][:], AX.X, ALU.add))
                    link(dve.reciprocal(lgs["rsum"][:], lgs["sum"][:]))
                    link(dve.tensor_tensor(lg["prob"][:], lg["exp"][:], over_experts(lgs["rsum"]), ALU.mult))
                    first_max(lg["prob"], lgs["max"], lgs["vmax"], lg["oh1"])
                    link(dve.scalar_tensor_tensor(out=lg["prob2"][:], in0=lg["oh1"][:], scalar=-2.0, in1=lg["prob"][:],
                                                  op0=ALU.mult, op1=ALU.add))
                    first_max(lg["prob2"], lgs["max2"], lgs["vmax2"], lg["oh2"])
                    link(dve.tensor_tensor(lg["both"][:], lg["oh1"][:], lg["oh2"][:], ALU.add))
                    link(dve.tensor_tensor(lg["prob2"][:], lg["prob"][:], lg["both"][:], ALU.mult))
                    link(dve.tensor_reduce(lgs["csum"][:], lg["prob2"][:], AX.X, ALU.add))
                    link(dve.reciprocal(lgs["rcsum"][:], lgs["csum"][:]))
                    link(dve.tensor_tensor(lg["comb"][:], lg["prob2"][:], over_experts(lgs["rcsum"]), ALU.mult))
                    link(dve.tensor_copy(comb3_b[:, :, 0, :], lg["comb"][:]))
                    link(dve.tensor_tensor(lg["rem"][:], lg["comb"][:], comb3_b[:, :, 0, :], ALU.subtract))
                    link(dve.tensor_copy(comb3_b[:, :, 1, :], lg["rem"][:]))
                    link(dve.tensor_tensor(comb3_b[:, :, 2, :], lg["rem"][:], comb3_b[:, :, 1, :], ALU.subtract))
                assert count[0] == GATE_OPS[l], count[0]

            def steps(t):
                for step in t.seg.steps:
                    kind, l, g = step[0], step[1], lag(step)
                    if kind == "ln":
                        normalise(t, l, g)
                    elif kind == "proj" and l == 0:
                        name, rotated = step[2][0], len(step[2]) == 2
                        dve.wait_ge(*W.filled(t, step))
                        dve.tensor_tensor((rope_b if rotated else rope_a)[name][:], W.bank(t, step)[:],
                                          (sin_s if rotated else cos_s)[:], ALU.mult).then_inc(W.free_sem(t, step), 1)
                    elif kind == "gate":
                        gate_chain(t, l, g, False)
                    elif kind == "gate2":
                        gate_chain(t, l, g, True)
                    elif kind == "v" and l == 1:
                        dve.wait_ge(*W.filled(t, step))
                        dve.tensor_tensor(v_ext[1][:, :, :, 0:DK], W.bank(t, step)[:].rearrange("p (k h d) -> p k h d", k=NBLK, h=HEADS),
                                          bv_s[:].rearrange("p (o h d) -> p o h d", o=1, h=HEADS).to_broadcast([P, NBLK, HEADS, DK]),
                                          ALU.add).then_inc(W.free_sem(t, step), 1)
                    elif kind == "bc":
                        e = step[2]
                        dve.wait_ge(*W.filled(t, step))
                        dve.tensor_tensor(x_e[e % 2][:], xnT[l][:], W.bank(t, step)[:], ALU.mult).then_inc(W.free_sem(t, step), 1)
                    elif kind == "s":
                        p, j, qb = step[2:]
                        grp = p // 2
                        if p % 2 == 0 and j == 0 and qb == 0 and grp >= 2:
                            dve.wait_ge(*neg_step[l](t, g, 4 * (grp - 1)))
                        dve.wait_ge(*S.filled(t, step))
                        dve.tensor_reduce(neg_max[grp % 2][:, j, p % 2, qb:qb + 1], S.bank(t, step)[:, 0:keys_of(l, qb)],
                                          AX.X, ALU.max, negate=True).then_inc(S.free_sem(t, step), 1)
                    elif kind == "silu":
                        if l == 0:
                            dve.wait_ge(*y_full[0](t, g))
                            dve.tensor_tensor(y_s[:], y_ps[:], xnT[0][:], ALU.add).then_inc(y_read.sem, 1)
                        dve.wait_ge(*tanh_done[l](t, g))
                        dve.tensor_scalar(y_sig[:], y_sig[:], 0.5, 0.5, ALU.mult, ALU.add).then_inc(sig_done[l].sem, 1)
                        if l == 1:
                            dve.wait_ge(*sig_done[1](t, g))
                            dve.tensor_tensor(g_s[1][:], y_ps[:], y_sig[:], ALU.mult).then_inc(g_done[1].sem, 1)
                    elif kind == "rcp":
                        c = step[2]
                        if c == 0:
                            dve.wait_ge(*o_moved[l](t, g, 16 * 8))
                        part = o_den[l][:, P * c:P * c + P]
                        dve.reciprocal(part, part).then_inc(rcp_done[l].sem, 1)
                    elif kind == "wo":
                        dve.wait_ge(*g_done[l](t, g))
                        dve.wait_ge(*W.filled(t, step))
                        if l == 0:
                            dve.tensor_tensor(g_s[0][:], W.bank(t, step)[:], g_s[0][:], ALU.mult).then_inc(W.free_sem(t, step), 1)
                        else:
                            dve.scalar_tensor_tensor(out=g_s[1][:], in0=W.bank(t, step)[:], scalar=bo_s[:, 0:1], in1=g_s[1][:],
                                                     op0=ALU.add, op1=ALU.mult).then_inc(W.free_sem(t, step), 1)
                    elif kind == "xT":
                        dve.wait_ge(*W.filled(t, step))
                        if l == 1:
                            dve.wait_ge(*out_stored(t, g, 0))
                            dve.wait_ge(*held(t, g))
                        elif LAST in t.seg.parts:
                            dve.wait_ge(*held(t, 1))
                        dve.tensor_tensor((x_mid, x_out)[l][:], W.bank(t, step)[:].rearrange("p (k d) -> p k d", k=NBLK),
                                          (x_in, x_hold)[l][:], ALU.add).then_inc(W.free_sem(t, step), 1)

            for seg in SEGMENTS:
                with iterations(dve, seg, (1, NBLK, GATE_OPS[0], GATE_OPS[1], 16, 4 * GROUPS, 16 * 8), ("work", "score")) as turn:
                    steps(turn)

        @block.gpsimd
        def _(pool):
            for tile in (k_ext[0], q_ext[0][0], q_ext[0][1]):
                nc.gpsimd.memset(tile[:].rearrange("p h n -> p (h n)").bitcast(F32), 0.0).then_inc(zeroed, 1)
            for l in LAYERS:
                nc.gpsimd.memset(v_ext[l][:], 1.0).then_inc(ones_set, 1)
            pool.wait_ge(consts_cast, N_CASTS)

            def steps(t):
                for step in t.seg.steps:
                    kind, l, g = step[0], step[1], lag(step)
                    if kind == "ln":
                        pool.wait_ge(*var_done[l](t, g))
                        nc.gpsimd.tensor_tensor(ln_rstd[l][:], ln_var[l][:], neg_half[:], ALU.pow).then_inc(rstd_done[l].sem, 1)
                    elif kind == "proj" and len(step[2]) == 2:
                        name = step[2][0]
                        pool.wait_ge(*W.emptied(t, ("proj", 0, name)))
                        pool.wait_ge(*W.emptied(t, step))
                        if name == "q" and LAST in t.seg.parts:
                            pool.wait_ge(*hi_done[1](t, 1, 2))
                        nc.gpsimd.tensor_tensor(full[name][:], rope_a[name][:], rope_b[name][:], ALU.add).then_inc(full_done.sem, 1)
                    elif kind == "hi":
                        i = "qk".index(step[2])
                        pool.wait_ge(*hi_done[l](t, g, i + 1))
                        nc.gpsimd.tensor_tensor(rest[step[2]][:], full[step[2]][:], parts[step[2]][:, 0, :], ALU.subtract)\
                          .then_inc(rest_done[l].sem, 1)
                    elif kind == "mid":
                        i = "qk".index(step[2])
                        pool.wait_ge(*mid_done[l](t, g, i + 1))
                        nc.gpsimd.tensor_tensor(parts[step[2]][:, 2, :], rest[step[2]][:], parts[step[2]][:, 1, :], ALU.subtract)\
                          .then_inc(lo_done[l].sem, 1)
                    elif kind == "mT":
                        grp = step[2]
                        i, k = grp % 2, 4 * grp
                        if grp >= 2:
                            pool.wait_ge(*W.filled(t, ("mT", l, grp - 2)))
                        maxima = S.emptied(t, ("s", l, 2 * grp + 1, 1, NBLK - 1))
                        pool.wait_ge(consts_cast, N_CASTS)
                        pool.wait_ge(*maxima)
                        nc.gpsimd.tensor_copy(neg3[i][:, :, 0, :, :], neg_max[i][:]).then_inc(neg_step[l].sem, 1)
                        pool.wait_ge(*neg_step[l](t, g, k + 1))
                        nc.gpsimd.tensor_tensor(neg_rest[i][:], neg_max[i][:], neg3[i][:, :, 0, :, :], ALU.subtract)\
                          .then_inc(neg_step[l].sem, 1)
                        rests = neg_step[l](t, g, k + 2)
                        pool.wait_ge(consts_cast, N_CASTS)
                        pool.wait_ge(*rests)
                        nc.gpsimd.tensor_copy(neg3[i][:, :, 1, :, :], neg_rest[i][:]).then_inc(neg_step[l].sem, 1)
                        pool.wait_ge(*neg_step[l](t, g, k + 3))
                        nc.gpsimd.tensor_tensor(neg3[i][:, :, 2, :, :], neg_rest[i][:], neg3[i][:, :, 1, :, :], ALU.subtract)\
                          .then_inc(neg_step[l].sem, 1)
                        if l == 1 and grp == 0:
                            mid_there = neg_step[1](t, g, 4)
                            pool.wait_ge(consts_cast, N_CASTS)
                            pool.wait_ge(*mid_there)
                            nc.gpsimd.tensor_copy(x_hold[:], x_mid[:]).then_inc(held.sem, 1)
                    elif kind == "st" and l == 0 and step[3] == 3:
                        kb = step[4]
                        exps = T.emptied(t, step)
                        pool.wait_ge(consts_cast, N_CASTS)
                        pool.wait_ge(*exps)
                        v = probs[:, kb, :, P * kb:P * kb + P]
                        nc.gpsimd.affine_select(out=v, in_=v, compare_op=ALU.is_ge, fill=0.0, base=0,
                                                pattern=[[0, 4], [1, P]], channel_multiplier=-1).then_inc(mask_done.sem, 1)
                    elif kind == "nrm":
                        pool.wait_ge(*rcp_done[l](t, g, NBLK))
                        nc.gpsimd.tensor_tensor(o_heads[l][:], o_heads[l][:], o_den[l][:], ALU.mult).then_inc(nrm_done[l].sem, 1)
                    elif kind == "silu" and l == 0:
                        pool.wait_ge(*sig_done[0](t, g))
                        nc.gpsimd.tensor_tensor(g_s[0][:], y_s[:], y_sig[:], ALU.mult).then_inc(g_done[0].sem, 1)

            for seg in SEGMENTS:
                with iterations(pool, seg, (1, 2, NBLK, 4 * GROUPS)) as turn:
                    steps(turn)


_ORDER = ["x", "wq0", "wq0r", "wk0", "wk0r", "wv0", "wo0", "gate0", "expert0", "wq1", "wk1", "wv1", "wo1", "gate1",
          "w1", "w2", "bq1", "bk1", "bv1", "bo1", "slopes", "cos_t", "sin_t", "ident", "causal", "rank", "select",
          "key_rows"]


def kernel(**inputs):
    import numpy as np
    import concourse.bacc as bacc
    from concourse.bass_utils import run_bass_kernel_spmd as run

    a = {k: np.asarray(v) for k, v in inputs.items()}

    def shaped(v):
        return np.ascontiguousarray(v)

    qk = np.array([(2 * p + j) * DK + d for j in range(2) for d in range(DK) for p in range(PAIRS)])
    swap = np.array([(2 * p + j) * DK + (d ^ 1) for j in range(2) for d in range(DK) for p in range(PAIRS)])
    oo = np.array([(4 * g + m) * DK + d for m in range(4) for d in range(DK) for g in range(GROUPS)])
    ins = {"x": shaped(a["L0_attn_x"].reshape(BATCH, NBLK, P, D).transpose(0, 2, 1, 3))}
    for l in LAYERS:
        t = f"L{l}_attn_"
        ins[f"wq{l}"] = shaped(a[t + "Wq"][qk].T)
        ins[f"wk{l}"] = shaped(a[t + "Wk"][qk].T)
        ins[f"wv{l}"] = shaped(a[t + "Wv"].T)
        ins[f"wo{l}"] = shaped(a[t + "Wo"].T[oo])
    ins["wq0r"] = shaped(a["L0_attn_Wq"][swap].T)
    ins["wk0r"] = shaped(a["L0_attn_Wk"][swap].T)
    ins["gate0"] = shaped(a["L0_ffn_gate_w"].T)
    ins["gate1"] = shaped(a["L1_ffn_Wg"])
    ins["expert0"] = shaped(a["L0_ffn_expert_w"].transpose(2, 0, 1))
    ins["w1"] = shaped(a["L1_ffn_W1"].transpose(1, 0, 2))
    ins["w2"] = shaped(a["L1_ffn_W2"].reshape(E, NF, P, D).transpose(2, 0, 1, 3))
    ins["bq1"] = shaped(a["L1_attn_bq"][qk][:, None])
    ins["bk1"] = shaped(a["L1_attn_bk"][qk][:, None])
    ins["bv1"] = shaped(np.broadcast_to(a["L1_attn_bv"][None, :], (P, D)))
    ins["bo1"] = shaped(a["L1_attn_bo"][:, None])
    ins["slopes"] = shaped(a["L1_attn_slopes"].reshape(PAIRS, 2).T.reshape(HEADS, 1))

    half = DK // 2
    inv_freq = np.float32(10000.0) ** (-np.arange(half, dtype=np.float32) * np.float32(2.0) / np.float32(DK))
    angles = np.arange(SEQ, dtype=np.float32)[None, :] * inv_freq.astype(np.float32)[:, None]
    d_of = np.array([d for j in range(2) for d in range(DK) for p in range(PAIRS)])
    sign = np.where(d_of % 2 == 0, -1.0, 1.0).astype(np.float32)[:, None]
    ins["cos_t"] = shaped(np.cos(angles.astype(np.float64)).astype(np.float32)[d_of // 2])
    ins["sin_t"] = shaped(np.sin(angles.astype(np.float64)).astype(np.float32)[d_of // 2] * sign)
    ins["ident"] = np.eye(P, dtype=np.float32)
    r = np.arange(P)
    ins["causal"] = np.where(r[None, :] > r[:, None], np.float32(MASKED), np.float32(0))
    ins["rank"] = shaped(np.broadcast_to((E - np.arange(E)).astype(np.float32), (P, NBLK, E)))
    sel = np.zeros((3 * E, E, P), np.float32)
    for e in range(E):
        sel[e::E, e, :] = 1.0
    ins["select"] = sel
    dist = np.arange(SEQ) - (SEQ - 1)
    far = (dist // P) * P
    rows = [far] * 3 + [dist - far] * 3 + [np.ones(SEQ)] * 3
    ins["key_rows"] = np.stack(rows).astype(np.float32)

    nc = bacc.Bacc("TRN2", target_bir_lowering=False, num_devices=1)
    args = [nc.dram_tensor(f"in_{n}", ins[n].shape, F32, kind="ExternalInput").ap() for n in _ORDER]
    out = nc.dram_tensor("out", (BATCH, P, NBLK, D), F32, kind="ExternalOutput").ap()
    two_layer_kernel(nc, *args, out)
    r = run(nc, [{f"in_{n}": ins[n] for n in _ORDER}], core_ids=[0])
    y = r.results[0]["out"]
    return np.ascontiguousarray(y.transpose(0, 2, 1, 3).reshape(BATCH, SEQ, D))
```

```python
from contextlib import ExitStack, contextmanager

import concourse.bass as bass
from concourse import mybir

F32 = mybir.dt.float32
BF16 = mybir.dt.bfloat16
ALU = mybir.AluOpType
ACT = mybir.ActivationFunctionType
AX = mybir.AxisListType

P = 128
BATCH, SEQ, D = 8, 512, 128
HEADS, DK = 16, 8
PAIRS, GROUPS = HEADS // 2, HEADS // 4
NBLK = SEQ // P
E = 8
F = 256
NF = F // P
LAYERS = (0, 1)
EPS = 1e-5
INV_SQRT_DK = 1.0 / float(DK) ** 0.5
MASKED = -1e30
TERMS = [(0, 0), (0, 1), (0, 2), (1, 0), (1, 1), (2, 0)]
BIAS_ROW = 2 * DK * len(TERMS)
MAX_ROW = P - 3
XE = 2
SPREAD = 4
VW = 32



def keys_of(l, qb):
    return P * (qb + 1) if l == 0 else SEQ


def first_query(l, kb):
    return P * kb if l == 0 else 0


def sides_in_bank(l, qb):
    return min(2, SEQ // keys_of(l, qb))


def members_in_bank(l, kb):
    return SEQ // (SEQ - first_query(l, kb))


SCORE_UNITS = (1.0, 1.583)
PERIOD = PAIRS * sum(SCORE_UNITS)
SCORES_AT = (0.0, PERIOD + PAIRS * SCORE_UNITS[0])
AT = {
    "probs0": 4.37, "probs1": 12.71, "neg": -0.06, "mT": 0.64, "pv0": 0.53, "pv1": 0.49,
    "front": {"load": 1.55, "ln": 2.6, "xn": 3.0, "xnT": 3.4, "q": 3.8, "qr": 3.95, "k": 4.29, "kr": 4.97,
              "gate": 4.78, "ohT": 5.46, "hi_q": 7.6, "hi_k": 8.0, "mid_q": 8.4, "mid_k": 9.36, "v": 13.66,
              "keep": 16.69, "silu": 22.1, "gmul": 22.49, "ext": 13.76, "ext_end": 16.48, "experts": 14.61,
              "experts_end": 22.26, "bc": 2.56, "xe": 0.79, "y": 0.0},
    "mid": {"rcp": 14.3, "rcp_end": 14.62, "nrm": 15.21, "wo": 15.36, "xT": 16.0, "ln": 16.31, "xn": 16.97,
            "xnT": 17.4, "q": 17.6, "gate": 17.65, "k": 17.8, "gexp": 17.71, "hi_q": 17.7, "hi_k": 17.95,
            "mid_q": 18.45, "mid_k": 18.7, "gate2": 18.05, "gate2_end": 20.5},
    "rear": {"ohT": 0.91, "v": 5.31, "hold": 8.96, "silu": 12.11, "gmul": 12.9, "ext": 4.87, "ext_end": 6.63,
             "experts": 2.71, "experts_end": 11.97, "bc": 2.5, "xe": 0.6, "h": 0.15, "y": 0.73},
    "last": {"rcp": 6.45, "rcp_end": 7.39, "nrm": 7.4, "wo": 7.71, "xT": 7.94},
}
PROBS_AT = (AT["probs0"], PERIOD + AT["probs1"])
FIRST = PROBS_AT[1] + 2 * (GROUPS - 1) * SCORE_UNITS[1] - 2 * PERIOD


def evenly(t0, t1, steps):
    return [(t0 + (t1 - t0) * n / len(steps), s) for n, s in enumerate(steps)]


def expert_steps(l, when):
    each, out = (when["experts_end"] - when["experts"]) / E, []
    for e in range(E):
        t = when["experts"] + e * each
        out += [(max(t - when["bc"], when["ohT"] + 0.2 + 0.02 * e), ("bc", l, e))]
        out += [(max(t - when["xe"], when["ohT"] + 0.75 + 0.02 * e), ("xe", l, e))]
        if l == 0:
            out += [(t + when["y"], ("y0", 0, e))]
        else:
            out += evenly(t + when["h"], t + when["h"] + each / 2, [("h", 1, e, f) for f in range(NF)])
            out += evenly(t + when["y"], t + when["y"] + each / 2, [("y1", 1, e, f) for f in range(NF)])
    return out


GATE_LINKS = (3, 5, 6, 5)


def timeline():
    at = []
    for l in LAYERS:
        unit, t0, t1 = SCORE_UNITS[l], SCORES_AT[l], PROBS_AT[l]
        for p in range(PAIRS):
            at += evenly(t0 + p * unit, t0 + (p + 1) * unit,
                         [("s", l, p, j, qb) for j in range(2) for qb in range(NBLK) if j % sides_in_bank(l, qb) == 0])
        for g in range(GROUPS):
            scored = t0 + 2 * (g + 1) * unit
            at += [(scored + AT["neg"], ("neg", l, g)), (scored + AT["mT"], ("mT", l, g))]
            t, quarter = t1 + 2 * g * unit, unit / 2
            for kb in range(NBLK):
                at += evenly(t + kb * quarter, t + (kb + 1) * quarter,
                             [("st", l, g, m, kb) for m in range(4) if (m + 1) % members_in_bank(l, kb) == 0])
                pv = t + (kb + 1) * quarter + AT[f"pv{l}"]
                if kb == NBLK - 1:
                    iteration_end = FIRST + PERIOD * (1 + (t + 2 * unit - 1e-3 - FIRST) // PERIOD)
                    pv = min(pv, iteration_end - 1e-4)
                at += [(pv, ("pv", l, g, kb))]
    front, mid, rear, last = AT["front"], AT["mid"], AT["rear"], AT["last"]
    early = [(front[k], (k, 0)) for k in ("load", "ln", "xn", "xnT", "gate", "ohT", "v", "keep", "silu", "gmul")]
    early += [(front[n], ("proj", 0, n)) for n in ("q", "qr", "k", "kr")]
    early += [(front[f"{k}_{n}"], (k, 0, n)) for k in ("hi", "mid") for n in "qk"]
    early += evenly(front["ext"], front["ext_end"], [("ext", 0, n) for n in range(len(TERMS))]) + expert_steps(0, front)
    at += [(t - PERIOD, s) for t, s in early]
    at += evenly(mid["rcp"], mid["rcp_end"], [("rcp", 0, c) for c in range(NBLK)])
    at += [(mid[k], (k, 0)) for k in ("nrm", "wo", "xT")] + [(mid[k], (k, 1)) for k in ("ln", "xn", "xnT", "gate", "gexp")]
    at += [(mid[n], ("proj", 1, n)) for n in "qk"] + [(mid[f"{k}_{n}"], (k, 1, n)) for k in ("hi", "mid") for n in "qk"]
    at += evenly(mid["gate2"], mid["gate2_end"], [("gate2", 1, n) for n in range(len(GATE_LINKS))])
    late = [(rear[k], (k, 1)) for k in ("ohT", "v", "hold", "silu", "gmul")]
    late += evenly(rear["ext"], rear["ext_end"], [("ext", 1, n) for n in range(len(TERMS))]) + expert_steps(1, rear)
    at += [(t + PERIOD, s) for t, s in late]
    end = evenly(last["rcp"], last["rcp_end"], [("rcp", 1, c) for c in range(NBLK)]) + [(last[k], (k, 1)) for k in ("nrm", "wo", "xT")]
    at += [(t + 2 * PERIOD, s) for t, s in end]
    return at


TIMELINE = timeline()
LAG = {s: int((t - FIRST) // PERIOD) for t, s in TIMELINE}
IN_ORDER = [s for _, s in sorted(((t - FIRST) % PERIOD, s) for t, s in TIMELINE)]


def lag(step):
    return LAG[step]


def has(first, end, lag):
    return 0 <= first - lag and end - 1 - lag < BATCH


def schedule(first, end):
    return [s for s in IN_ORDER if has(first, end, lag(s))]


W_KINDS = ("xnT", "proj", "gate", "v", "ohT", "h", "mT", "wo", "xT")


class Segment:

    def __init__(self, first, end, before):
        self.first, self.end = first, end
        self.steps = schedule(first, end)
        self.uses, self.offset = {}, dict(before)
        for ring, kinds in (("work", W_KINDS), ("score", ("s",)), ("scoreT", ("st",))):
            self.uses[ring] = {s: n for n, s in enumerate(s for s in self.steps if s[0] in kinds)}
            before[ring] += len(self.uses[ring]) * (end - first)
        assert end - first == 1 or all(len(u) % 2 == 0 for u in self.uses.values())


def segments():
    before = {"work": 0, "score": 0, "scoreT": 0}
    lags = set(LAG.values())
    edges = list(range(min(lags), max(lags) + 1)) + list(range(BATCH + min(lags), BATCH + max(lags) + 1))
    return [Segment(first, end, before) for first, end in zip(edges, edges[1:])]


class Turn:

    def __init__(self, eng, seg, i, rises, rings):
        self.eng, self.seg, self.i, self.bases, self.waits = eng, seg, i, {}, 0
        self.looped = seg.end - seg.first > 1
        if self.looped:
            self.scratch = [eng.alloc_register(f"wait_value{n}") for n in range(8)]
            for per in sorted(set(rises) | {len(uses) // 2 for ring, uses in seg.uses.items() if ring in rings}):
                self.bases[per] = eng.alloc_register(f"iteration_times_{per}")
                eng.reg_mul(self.bases[per], i, per)

    def has(self, lag):
        return has(self.seg.first, self.seg.end, lag)

    def value(self, per, const):
        if not self.looped:
            assert self.i * per + const > 0
            return self.i * per + const
        assert self.seg.first * per + const > 0
        if const == 0:
            return self.bases[per]
        reg = self.scratch[self.waits % len(self.scratch)]
        self.waits += 1
        self.eng.reg_add(reg, self.bases[per], const)
        return reg


@contextmanager
def iterations(eng, seg, rises, rings=("work", "score", "scoreT")):
    if seg.end - seg.first > 1:
        with eng.Fori(seg.first, seg.end) as i:
            yield Turn(eng, seg, i, rises, rings)
    else:
        yield Turn(eng, seg, seg.first, (), ())


class Signal:

    def __init__(self, ctx, nc, name, per=1, credit=0):
        self.sem = ctx.enter_context(nc.semaphore(name))
        self.per, self.credit = per, credit

    def __call__(self, turn, lag, k=1):
        return self.sem, turn.value(self.per, self.credit + k - lag * self.per)


class Ring:

    def __init__(self, ctx, nc, name):
        self.name = name
        self.banks = [ctx.enter_context(nc.psum_tensor(f"{name}{i}", [P, SEQ], F32)) for i in range(2)]
        self.full = [ctx.enter_context(nc.semaphore(f"{name}_full{i}")) for i in range(2)]
        self.free = [ctx.enter_context(nc.semaphore(f"{name}_free{i}")) for i in range(2)]

    def place(self, turn, step):
        return turn.seg.offset[self.name] + turn.seg.uses[self.name][step]

    def count(self, turn, step, extra):
        per = len(turn.seg.uses[self.name]) // 2 if turn.looped else 0
        return turn.value(per, self.place(turn, step) // 2 + 1 + extra - per * turn.seg.first)

    def bank(self, turn, step):
        return self.banks[self.place(turn, step) % 2]

    def filled(self, turn, step):
        return self.full[self.place(turn, step) % 2], self.count(turn, step, 0)

    def freed(self, turn, step):
        return self.free[self.place(turn, step) % 2], self.count(turn, step, 0)

    def emptied(self, turn, step):
        return self.free[self.place(turn, step) % 2], self.count(turn, step, 1)

    def full_sem(self, turn, step):
        return self.full[self.place(turn, step) % 2]

    def free_sem(self, turn, step):
        return self.free[self.place(turn, step) % 2]


def two_layer_kernel(nc, x, wq0, wq0r, wk0, wk0r, wv0, wo0, gate0, expert0, wq1, wk1, wv1, wo1, gate1, w1, w2,
                     bq1, bk1, bv1, bo1, slopes, cos_t, sin_t, ident, causal, rank, key_rows, out):
    ctx = ExitStack()
    with ctx:
        def sb(name, shape, dt=F32):
            return ctx.enter_context(nc.sbuf_tensor(name, shape, dt))

        def sig(name, per=1, credit=0):
            return Signal(ctx, nc, name, per, credit)

        proj_w = {(0, "q"): sb("wq0_s", [P, D]), (0, "qr"): sb("wq0r_s", [P, D]), (0, "k"): sb("wk0_s", [P, D]),
                  (0, "kr"): sb("wk0r_s", [P, D]), (1, "q"): sb("wq1_s", [P, D]), (1, "k"): sb("wk1_s", [P, D])}
        wv_s = [sb("wv0_s", [P, D]), sb("wv1_s", [P, D])]
        wo_s = [sb("wo0_s", [P, D]), sb("wo1_s", [P, D])]
        gate_s = [sb("gate0_s", [P, E]), sb("gate1_s", [P, E])]
        expert_s = sb("expert_s", [P, E, D])
        w1_s = sb("w1_s", [P, E, F])
        w2_s = sb("w2_s", [P, E, NF, D])
        bq_s, bk_s, bo_s = sb("bq_s", [P, 1]), sb("bk_s", [P, 1]), sb("bo_s", [P, 1])
        bv_s = sb("bv_s", [P, D])
        cos_s, sin_s = sb("cos_s", [P, SEQ]), sb("sin_s", [P, SEQ])
        ident_s, identb_s = sb("ident_s", [P, P]), sb("identb_s", [P, P], BF16)
        causalb_s = sb("causalb_s", [P, P], BF16)
        rank_s = sb("rank_s", [P, NBLK, E])
        slope_s, slope3_s = sb("slope_s", [HEADS, 4]), sb("slope3_s", [HEADS, 3], BF16)
        neg_half = sb("neg_half", [P, NBLK])

        x_in, x_keep, x_mid, x_hold, x_out = (sb(n, [P, NBLK, D]) for n in ("x_in", "x_keep", "x_mid", "x_hold", "x_out"))
        ln_src = (x_in, x_mid)
        ln_stat = [sb(f"ln_stat{l}", [P, NBLK, 6]) for l in LAYERS]
        ln_mv = [sb(f"ln_mv{l}", [P, NBLK, 2]) for l in LAYERS]
        ln_var = [sb(f"ln_var{l}", [P, NBLK]) for l in LAYERS]
        ln_rstd = [sb(f"ln_rstd{l}", [P, NBLK]) for l in LAYERS]
        xn = sb("xn", [P, NBLK, D])
        xnT = [sb(f"xnT{l}", [P, SEQ]) for l in LAYERS]
        rope_a = {n: sb(f"rope_a_{n}", [P, SEQ]) for n in "qk"}
        rope_b = {n: sb(f"rope_b_{n}", [P, SEQ]) for n in "qk"}
        full = rope_b
        rest = rope_a
        parts = {n: sb(f"parts_{n}", [P, 3, SEQ], BF16) for n in "qk"}
        k_ext = [sb(f"k_ext{l}", [P, PAIRS, SEQ], BF16) for l in LAYERS]
        q_ext = [[sb(f"q_ext{l}_{j}", [P, PAIRS, SEQ], BF16) for j in range(2)] for l in LAYERS]
        v_ext = [sb(f"v_ext{l}", [P, NBLK, HEADS, VW]) for l in LAYERS]
        neg_max = [sb(f"neg_max{i}", [P, 2, 2, NBLK]) for i in range(2)]
        neg_rest = [sb(f"neg_rest{i}", [P, 2, 2, NBLK]) for i in range(2)]
        neg3 = [sb(f"neg3_{i}", [P, 2, 3, 2, NBLK], BF16) for i in range(2)]
        NEG_ROWS = 3 * 2 * NBLK
        neg_row = [sb(f"neg_row{i}", [2 * NEG_ROWS, P], BF16) for i in range(2)]
        probs = sb("probs", [P, NBLK, 4, SEQ])
        stage = probs[:].rearrange("p k m n -> p (k m n)")
        keyrow_s = stage[0:9, 1024:1536]
        keyrowb_s = stage[0:9, 1536:1792].bitcast(BF16)
        sloperow_s = stage[0:HEADS, 3584:4352].bitcast(BF16).rearrange("p (a n) -> p a n", a=3)
        causal_s = stage[:, 4352:4352 + P]
        o_quad = sb("o_quad", [P, GROUPS, SEQ])
        o_heads = [sb(f"o_heads{l}", [P, SEQ]) for l in LAYERS]
        o_den = [sb(f"o_den{l}", [P, SEQ]) for l in LAYERS]
        lg = {n: sb(f"g_{n}", [P, NBLK, E]) for n in
              ("logit", "eq", "val", "oh1", "oh2", "exp", "prob", "prob2", "both")}
        g_shift = sb("g_shift", [P, NBLK, E])
        lgs = {n: sb(f"gs_{n}", [P, NBLK]) for n in
               ("max", "vmax", "sum", "rsum", "max2", "vmax2", "csum", "rcsum")}
        weight = [sb(f"weight{l}", [P, NBLK, E]) for l in LAYERS]
        ohT = [sb(f"ohT{l}", [E, SEQ]) for l in LAYERS]
        spread_w = [sb(f"spread_w{i}", [P, SEQ]) for i in range(SPREAD)]
        x_e = [sb(f"x_e{i}", [P, SEQ]) for i in range(XE)]
        hid = [sb(f"hid{i}", [P, SEQ]) for i in range(2)]
        y_sig = sb("y_sig", [P, SEQ])
        g_s = [sb(f"g_s{l}", [P, SEQ]) for l in LAYERS]

        W, S, T = Ring(ctx, nc, "work"), Ring(ctx, nc, "score"), Ring(ctx, nc, "scoreT")
        o_ps = ctx.enter_context(nc.psum_tensor("o_ps", [P, SEQ], F32))
        y_ps = ctx.enter_context(nc.psum_tensor("y_ps", [P, SEQ], F32))

        def per_layer(name, per=1):
            return [sig(f"{name}_{l}", per) for l in LAYERS]

        first_in, staged_in, rest_in, consts_cast, slope_step, zeroed, ones_set, static_rows = (
            ctx.enter_context(nc.semaphore(n)) for n in
            ("first_in", "staged_in", "rest_in", "consts_cast", "slope_step", "zeroed", "ones_set", "static_rows"))
        x_loaded = sig("x_loaded", 16)
        stat_done, aggr_done = per_layer("stat_done", NBLK), per_layer("aggr_done", NBLK)
        var_done, rstd_done, xn_done = per_layer("var_done"), per_layer("rstd_done"), per_layer("xn_done")
        full_done = sig("full_done", 2)
        hi_done, rest_done, mid_done, lo_done = (per_layer(n, 2) for n in ("hi_done", "rest_done", "mid_done", "lo_done"))
        EXT_DMAS = 3 * len(TERMS)
        ext_done = per_layer("ext_done", 16 * EXT_DMAS)
        GATE_OPS = (5, 2 + sum(GATE_LINKS))
        gate_step = [sig(f"gate_step_{l}", GATE_OPS[l]) for l in LAYERS]
        gate_exp = sig("gate_exp")
        spread_in = [[sig(f"spread_in{l}_{i}", 16 * E // SPREAD) for i in range(SPREAD)] for l in LAYERS]
        xe_done = per_layer("xe_done", E)
        y0_step = sig("y0_step", E)
        y_full = sig("y_full")
        neg_step = per_layer("neg_step", 4 * GROUPS)
        mrow_in = [[sig(f"mrow_in{l}_{i}", 32 * GROUPS // 2) for i in range(2)] for l in LAYERS]
        mask_done = sig("mask_done", GROUPS * NBLK)
        pv_done = per_layer("pv_done", GROUPS)
        o_out = per_layer("o_out", GROUPS)
        o_moved = per_layer("o_moved", 16 * 8)
        rcp_done, nrm_done = per_layer("rcp_done", NBLK), per_layer("nrm_done")
        y_read, tanh_done, sig_done, g_done = sig("y_read"), per_layer("tanh_done"), per_layer("sig_done"), per_layer("g_done")
        kept, held = sig("kept"), sig("held")
        out_stored = sig("out_stored", 16, credit=16)

        LOADS = [[(ident_s[:], ident), (proj_w[0, "q"][:], wq0), (proj_w[0, "qr"][:], wq0r), (proj_w[0, "k"][:], wk0),
                  (proj_w[0, "kr"][:], wk0r), (gate_s[0][:], gate0), (cos_s[:], cos_t), (sin_s[:], sin_t),
                  (rank_s[:], rank), (wv_s[0][:], wv0)],
                 [(causal_s, causal), (keyrow_s, key_rows), (slope_s[:, 0:1], slopes)],
                 [(expert_s[:], expert0), (wo_s[0][:], wo0), (proj_w[1, "q"][:], wq1), (proj_w[1, "k"][:], wk1),
                  (bq_s[:], bq1), (bk_s[:], bk1), (gate_s[1][:], gate1), (wv_s[1][:], wv1), (bv_s[:], bv1),
                  (w1_s[:], w1), (w2_s[:], w2), (wo_s[1][:], wo1), (bo_s[:], bo1)]]
        N_FIRST, N_STAGED, N_REST = (16 * len(group) for group in LOADS)
        N_CASTS = 5
        N_ZERO = 6
        N_STATIC = 16 * (3 + 2 * 6)
        SEGMENTS = segments()

        def before_group(t, l, grp, g):
            if grp >= 2:
                return [(l, grp - 2, g)]
            other = (0, grp + 2, g - 1) if l == 1 else (1, grp + 2, g + 2)
            same = (l, grp + 2, g + 1)
            return [c for c in (other, same) if t.has(c[2])][:1]

        def before_expert(t, l, e, g, depth):
            if e >= depth:
                return [(l, e - depth, g)]
            other = (0, E - depth + e, g - 1) if l == 1 else (1, E - depth + e, g + 2)
            return [c for c in (other, (l, E - depth + e, g + 1)) if t.has(c[2])][:1]

        def before_layer(t, l, g):
            other = (0, g - 1) if l == 1 else (1, g + 2)
            return [c for c in (other, (l, g + 1)) if t.has(c[1])][:1]

        block = ctx.enter_context(nc.Block())

        @block.sync
        def _(sp):
            sp.dma_start(x_in[:], x[0]).then_inc(x_loaded.sem, 16)
            for group, loaded in zip(LOADS, (first_in, staged_in, rest_in)):
                for dst, src in group:
                    sp.dma_start(dst, src).then_inc(loaded, 16)
            sp.wait_ge(zeroed, N_ZERO)
            sp.wait_ge(consts_cast, N_CASTS)
            over_pairs = lambda rows: keyrowb_s[rows].unsqueeze(1).to_broadcast([rows.stop - rows.start, PAIRS, SEQ])
            for l in LAYERS:
                sp.dma_start(k_ext[l][MAX_ROW:P], over_pairs(slice(6, 9))).then_inc(static_rows, 16)
            sp.dma_start(k_ext[1][BIAS_ROW:BIAS_ROW + 6], over_pairs(slice(0, 6))).then_inc(static_rows, 16)
            for n in range(6):
                for j in range(2):
                    sp.dma_start(q_ext[1][j][BIAS_ROW + n:BIAS_ROW + n + 1], sloperow_s[PAIRS * j:PAIRS * (j + 1), n % 3, :])\
                      .then_inc(static_rows, 16)

            for seg in SEGMENTS:
                with iterations(sp, seg, (1, 2, NBLK, E), ("work", "scoreT")) as t:
                    for step in seg.steps:
                        kind, l, g = step[0], step[1], lag(step)
                        if kind == "ext":
                            n = step[2]
                            waits = []
                            if n == 0:
                                waits.append(lo_done[l](t, g, 2))
                                if t.has(g + 1):
                                    waits.append(T.filled(t, ("st", l, GROUPS - 1, 3, NBLK - 1)))
                            for wait in waits:
                                sp.wait_ge(*wait)
                            qp, kp = TERMS[n]
                            row = 2 * DK * n
                            sp.dma_start(k_ext[l][row:row + 2 * DK], parts["k"][:, kp, :]).then_inc(ext_done[l].sem, 16)
                            for j in range(2):
                                sp.dma_start(q_ext[l][j][row + DK * j:row + DK * j + DK],
                                             parts["q"][64 * j:64 * j + 64, qp, :]).then_inc(ext_done[l].sem, 16)
                        elif kind == "bc":
                            e = step[2]
                            waits = [xe_done[l2](t, g2, e2 + 1) for l2, e2, g2 in before_expert(t, l, e, g, SPREAD)]
                            if e == 0:
                                waits.append(W.emptied(t, ("ohT", l)))
                            sp.wait_ge(first_in, N_FIRST)
                            for wait in waits:
                                sp.wait_ge(*wait)
                            sp.dma_start(spread_w[e % SPREAD][:], ohT[l][e:e + 1, :].unsqueeze(1).to_broadcast([1, P, SEQ]))\
                              .then_inc(spread_in[l][e % SPREAD].sem, 16)
                        elif kind == "mT":
                            grp = step[2]
                            sp.wait_ge(*W.emptied(t, step))
                            for j in range(2):
                                dst = q_ext[l][j][MAX_ROW:P, 2 * grp:2 * grp + 2, :].rearrange("r a (k n) -> r (a k) n", k=NBLK)
                                sp.dma_start(dst, neg_row[grp % 2][NEG_ROWS * j:NEG_ROWS * (j + 1), :])\
                                  .then_inc(mrow_in[l][grp % 2].sem, 16)
                        elif kind == "pv" and step[2:] == (GROUPS - 1, NBLK - 1):
                            sp.wait_ge(*o_out[l](t, g, GROUPS))
                            for m in range(4):
                                to = slice(32 * m, 32 * m + 32)
                                sp.dma_start(o_heads[l][to], o_quad[32 * m:32 * m + DK]).then_inc(o_moved[l].sem, 16)
                                sp.dma_start(o_den[l][to], o_quad[32 * m + DK:32 * m + 2 * DK]).then_inc(o_moved[l].sem, 16)
                        elif kind == "load" and seg.first >= 0:
                            if t.has(g + 1):
                                copied = kept(t, g + 1)
                                sp.wait_ge(zeroed, N_ZERO)
                                sp.wait_ge(*copied)
                            sp.dma_start(x_in[:], x[t.i - g]).then_inc(x_loaded.sem, 16)
                        elif kind == "xT" and l == 1:
                            sum_done = W.emptied(t, step)
                            sp.wait_ge(zeroed, N_ZERO)
                            sp.wait_ge(*sum_done)
                            sp.dma_start(out[t.i - g], x_out[:]).then_inc(out_stored.sem, 16)
            sp.wait_ge(out_stored.sem, out_stored.credit + 16 * BATCH)

        @block.tensor
        def _(pe):
            pe.wait_ge(first_in, N_FIRST)

            def steps(t):
                for step in t.seg.steps:
                    kind, l, g = step[0], step[1], lag(step)
                    if kind in W_KINDS:
                        bank = W.bank(t, step)
                        bank_b = bank[:].bitcast(BF16)
                        full_sem = W.full_sem(t, step)
                    if t.seg.first == -1:
                        if step == ("y0", 0, 0):
                            pe.wait_ge(rest_in, N_REST)
                        elif step == ("s", 0, 0, 0, 0):
                            pe.wait_ge(static_rows, N_STATIC)
                            pe.wait_ge(ones_set, 2)
                            pe.wait_ge(consts_cast, N_CASTS)
                    if kind == "xnT":
                        pe.wait_ge(*xn_done[l](t, g))
                        pe.wait_ge(*W.freed(t, step))
                        for k in range(NBLK):
                            mm = pe.transpose(bank[:, P * k:P * k + P], xn[:, k, :], ident_s[:])
                        mm.then_inc(full_sem, 1)
                    elif kind == "proj":
                        pe.wait_ge(*W.emptied(t, ("xnT", l)))
                        pe.wait_ge(*W.freed(t, step))
                        pe.matmul(bank[:], proj_w[l, step[2]][:], xnT[l][:], start=True, stop=True).then_inc(full_sem, 1)
                    elif kind in ("gate", "v"):
                        rhs, n = (gate_s[l], E) if kind == "gate" else (wv_s[l], P)
                        if kind == "gate" or l == 0:
                            pe.wait_ge(*W.emptied(t, ("xnT", l)))
                        pe.wait_ge(*W.freed(t, step))
                        for k in range(NBLK):
                            mm = pe.matmul(bank[:, n * k:n * k + n], xnT[l][:, P * k:P * k + P], rhs[:], start=True, stop=True)
                        mm.then_inc(full_sem, 1)
                    elif kind == "ohT":
                        pe.wait_ge(*gate_step[l](t, g, GATE_OPS[l]))
                        pe.wait_ge(*W.freed(t, step))
                        for k in range(NBLK):
                            mm = pe.transpose(bank[0:E, P * k:P * k + P], weight[l][:, k, :], ident_s[:])
                        mm.then_inc(full_sem, 1)
                    elif kind == "y0":
                        e = step[2]
                        pe.wait_ge(*xe_done[0](t, g, e + 1))
                        if e == 0 and t.has(1):
                            pe.wait_ge(*g_done[1](t, 1))
                        mm = pe.matmul(y_ps[:], expert_s[:, e, :], x_e[e % 2][:], start=e == 0, stop=e == E - 1)
                        mm.then_inc(y0_step.sem, 1)
                    elif kind == "h":
                        e, f = step[2:]
                        if f == 0:
                            pe.wait_ge(*xe_done[1](t, g, e + 1))
                        pe.wait_ge(*W.freed(t, step))
                        pe.matmul(bank[:], w1_s[:, e, P * f:P * f + P], x_e[e % 2][:], start=True, stop=True).then_inc(full_sem, 1)
                    elif kind == "y1":
                        e, f = step[2:]
                        pe.wait_ge(*W.emptied(t, ("h", 1, e, f)))
                        if e == 0 and f == 0 and t.has(0):
                            pe.wait_ge(*y_read(t, 0))
                        mm = pe.matmul(y_ps[:], w2_s[:, e, f, :], hid[f][:], start=e == 0 and f == 0, stop=e == E - 1 and f == NF - 1)
                        if e == E - 1 and f == NF - 1:
                            mm.then_inc(y_full.sem, 1)
                    elif kind == "s":
                        p, j, qb = step[2:]
                        if p == 0 and j == 0 and qb == 0:
                            pe.wait_ge(*ext_done[l](t, g, 16 * EXT_DMAS))
                        pe.wait_ge(*S.freed(t, step))
                        n, bank = keys_of(l, qb), S.bank(t, step)
                        for side in range(j, j + sides_in_bank(l, qb)):
                            c = n * (side - j)
                            mm = pe.matmul(bank[:, c:c + n], q_ext[l][side][0:MAX_ROW, p, P * qb:P * qb + P],
                                           k_ext[l][0:MAX_ROW, p, 0:n], start=True, stop=l == 1)
                            if l == 0:
                                mm = pe.matmul(bank[:, c + P * qb:c + n], identb_s[:], causalb_s[:], start=False, stop=True)
                        mm.then_inc(S.full_sem(t, step), 1)
                    elif kind == "mT":
                        grp = step[2]
                        split, freed = neg_step[l](t, g, 4 * grp + 4), W.freed(t, step)
                        pe.wait_ge(consts_cast, N_CASTS)
                        pe.wait_ge(*split)
                        pe.wait_ge(*freed)
                        pe.transpose(bank_b[0:2 * NEG_ROWS, 0:P], neg3[grp % 2][:].rearrange("p j a b k -> p (j a b k)"), identb_s[:])\
                          .then_inc(full_sem, 1)
                    elif kind == "st":
                        grp, m, kb = step[2:]
                        if m == 0 and kb == 0:
                            pe.wait_ge(*mrow_in[l][grp % 2](t, g, 32 * (grp // 2 + 1)))
                        pe.wait_ge(*T.freed(t, step))
                        n, heads = SEQ - first_query(l, kb), members_in_bank(l, kb)
                        for c, member in enumerate(range(m + 1 - heads, m + 1)):
                            p, j = 2 * grp + member // 2, member % 2
                            mm = pe.matmul(T.bank(t, step)[:, n * c:n * c + n], k_ext[l][:, p, P * kb:P * kb + P],
                                           q_ext[l][j][:, p, SEQ - n:SEQ], start=True, stop=True)
                        mm.then_inc(T.full_sem(t, step), 1)
                    elif kind == "pv":
                        grp, kb = step[2:]
                        if l == 0:
                            pe.wait_ge(*mask_done(t, g, NBLK * grp + kb + 1))
                        pe.wait_ge(*T.emptied(t, ("st", l, grp, 3, kb)))
                        if kb == 0 and grp > 0:
                            pe.wait_ge(*o_out[l](t, g, grp))
                        if kb == 0 and grp == 0:
                            for l2, g2 in before_layer(t, l, g):
                                pe.wait_ge(*o_out[l2](t, g2, GROUPS))
                        n = first_query(l, kb)
                        for m in range(4):
                            mm = pe.matmul(o_ps[32 * m:32 * m + VW, n:SEQ], v_ext[l][:, kb, 4 * grp + m, :],
                                           probs[:, kb, m, n:SEQ], start=kb == 0, stop=kb == NBLK - 1)
                        if kb == NBLK - 1:
                            mm.then_inc(pv_done[l].sem, 1)
                    elif kind == "wo":
                        pe.wait_ge(*nrm_done[l](t, g))
                        pe.wait_ge(*W.freed(t, step))
                        pe.matmul(bank[:], wo_s[l][:], o_heads[l][:], start=True, stop=True).then_inc(full_sem, 1)
                    elif kind == "xT":
                        pe.wait_ge(*W.emptied(t, ("wo", l)))
                        pe.wait_ge(*W.freed(t, step))
                        for k in range(NBLK):
                            mm = pe.transpose(bank[:, P * k:P * k + P], g_s[l][:, P * k:P * k + P], ident_s[:])
                        mm.then_inc(full_sem, 1)

            for seg in SEGMENTS:
                with iterations(pe, seg, (1, NBLK, E, GATE_OPS[0], GATE_OPS[1], 4 * GROUPS, 16 * GROUPS, 16 * EXT_DMAS)) as turn:
                    steps(turn)

        @block.scalar
        def _(act):
            act.wait_ge(ones_set, 2)

            def steps(t):
                for step in t.seg.steps:
                    kind, l, g = step[0], step[1], lag(step)
                    if t.seg.first == 0 and step == ("st", 0, 0, 0, 0):
                        act.wait_ge(static_rows, N_STATIC)
                        act.wait_ge(rest_in, N_REST)
                    if kind == "xnT":
                        act.wait_ge(*W.filled(t, step))
                        nc.scalar.copy(xnT[l][:], W.bank(t, step)[:]).then_inc(W.free_sem(t, step), 1)
                    elif kind == "proj" and l == 1:
                        bias = {"q": bq_s, "k": bk_s}[step[2]]
                        if step[2] == "q" and t.has(-1):
                            act.wait_ge(*rest_done[0](t, -1, 2))
                        act.wait_ge(*W.filled(t, step))
                        nc.scalar.activation(full[step[2]][:], W.bank(t, step)[:], ACT.Identity, bias=bias[:, 0:1])\
                          .then_inc(W.free_sem(t, step), 1)
                    elif kind == "hi":
                        i = "qk".index(step[2])
                        if i == 0 and l == 1 and t.has(-1):
                            act.wait_ge(*ext_done[0](t, -1, 16 * EXT_DMAS))
                        if i == 0 and l == 0 and t.has(1):
                            act.wait_ge(*ext_done[1](t, 1, 16 * EXT_DMAS))
                        act.wait_ge(*(full_done(t, g, i + 1) if l == 0 else W.emptied(t, ("proj", 1, step[2]))))
                        nc.scalar.copy(parts[step[2]][:, 0, :], full[step[2]][:]).then_inc(hi_done[l].sem, 1)
                    elif kind == "mid":
                        i = "qk".index(step[2])
                        act.wait_ge(*rest_done[l](t, g, i + 1))
                        nc.scalar.copy(parts[step[2]][:, 1, :], rest[step[2]][:]).then_inc(mid_done[l].sem, 1)
                    elif kind == "v" and l == 0:
                        if t.has(g + 1):
                            act.wait_ge(*pv_done[0](t, g + 1, GROUPS))
                        act.wait_ge(*W.filled(t, step))
                        nc.scalar.copy(v_ext[0][:, :, :, 0:DK], W.bank(t, step)[:].rearrange("p (k h d) -> p k h d", k=NBLK, h=HEADS))\
                          .then_inc(W.free_sem(t, step), 1)
                    elif kind == "gexp":
                        act.wait_ge(*gate_step[1](t, g, 2))
                        nc.scalar.activation(lg["exp"][:], g_shift[:], ACT.Exp).then_inc(gate_exp.sem, 1)
                    elif kind == "ohT":
                        act.wait_ge(*W.filled(t, step))
                        if t.has(g + 1):
                            act.wait_ge(*xe_done[l](t, g + 1, E))
                        nc.scalar.copy(ohT[l][:], W.bank(t, step)[0:E, :]).then_inc(W.free_sem(t, step), 1)
                    elif kind == "h":
                        act.wait_ge(*W.filled(t, step))
                        nc.scalar.activation(hid[step[3]][:], W.bank(t, step)[:], ACT.Relu).then_inc(W.free_sem(t, step), 1)
                    elif kind == "mT":
                        grp = step[2]
                        act.wait_ge(*W.filled(t, step))
                        for l2, grp2, g2 in before_group(t, l, grp, g):
                            act.wait_ge(*mrow_in[l2][grp % 2](t, g2, 32 * (grp2 // 2 + 1)))
                        nc.scalar.copy(neg_row[grp % 2][:], W.bank(t, step)[:].bitcast(BF16)[0:2 * NEG_ROWS, 0:P])\
                          .then_inc(W.free_sem(t, step), 1)
                    elif kind == "st":
                        grp, m, kb = step[2:]
                        n, heads = SEQ - first_query(l, kb), members_in_bank(l, kb)
                        act.wait_ge(*T.filled(t, step))
                        nc.scalar.activation(probs[:, kb, m + 1 - heads:m + 1, SEQ - n:SEQ],
                                             T.bank(t, step)[:, 0:n * heads].rearrange("p (m n) -> p m n", m=heads), ACT.Exp,
                                             scale=INV_SQRT_DK).then_inc(T.free_sem(t, step), 1)
                    elif kind == "pv" and step[3] == NBLK - 1:
                        grp = step[2]
                        act.wait_ge(*pv_done[l](t, g, grp + 1))
                        if grp == 0:
                            for l2, g2 in before_layer(t, l, g):
                                act.wait_ge(*o_moved[l2](t, g2, 16 * 8))
                        nc.scalar.copy(o_quad[:, grp, :], o_ps[:]).then_inc(o_out[l].sem, 1)
                    elif kind == "silu":
                        if l == 0:
                            act.wait_ge(*y_read(t, g))
                        else:
                            act.wait_ge(*y_full(t, g))
                        nc.scalar.activation(y_sig[:], (g_s[0] if l == 0 else y_ps)[:], ACT.Tanh, scale=0.5).then_inc(tanh_done[l].sem, 1)

            for seg in SEGMENTS:
                with iterations(act, seg, (1, 2, NBLK, E, GATE_OPS[1], 16 * GROUPS, 16 * 8, 16 * EXT_DMAS), ("work", "scoreT")) as turn:
                    steps(turn)

        @block.vector
        def _(dve):
            dve.sem_inc(out_stored.sem, 16)
            for ring in (W, S, T):
                for i in range(2):
                    dve.sem_inc(ring.free[i], 1)
            for tile in (k_ext[1], q_ext[1][0], q_ext[1][1]):
                dve.memset(tile[:].rearrange("p h n -> p (h n)").bitcast(F32), 0.0).then_inc(zeroed, 1)
            dve.memset(neg_half[:], -0.5).then_inc(consts_cast, 1)
            dve.wait_ge(first_in, N_FIRST)
            dve.tensor_copy(identb_s[:], ident_s[:]).then_inc(consts_cast, 1)

            def set_up_scores():
                dve.wait_ge(staged_in, N_STAGED)
                dve.tensor_scalar(slope_s[:, 1:2], slope_s[:, 0:1], float(DK) ** 0.5, None, ALU.mult).then_inc(slope_step, 1)
                dve.wait_ge(slope_step, 1)
                dve.tensor_copy(slope3_s[:, 0:1], slope_s[:, 1:2]).then_inc(slope_step, 1)
                dve.wait_ge(slope_step, 2)
                dve.tensor_tensor(slope_s[:, 2:3], slope_s[:, 1:2], slope3_s[:, 0:1], ALU.subtract).then_inc(slope_step, 1)
                dve.wait_ge(slope_step, 3)
                dve.tensor_copy(slope3_s[:, 1:2], slope_s[:, 2:3]).then_inc(slope_step, 1)
                dve.wait_ge(slope_step, 4)
                dve.tensor_tensor(slope3_s[:, 2:3], slope_s[:, 2:3], slope3_s[:, 1:2], ALU.subtract).then_inc(slope_step, 1)
                dve.wait_ge(slope_step, 5)
                dve.tensor_copy(sloperow_s, slope3_s[:].unsqueeze(2).to_broadcast([HEADS, 3, SEQ])).then_inc(consts_cast, 1)
                for dst, src in ((keyrowb_s, keyrow_s), (causalb_s[:], causal_s)):
                    dve.tensor_copy(dst, src).then_inc(consts_cast, 1)

            def over_experts(t):
                return t[:].unsqueeze(2).to_broadcast([P, NBLK, E])

            def ln_variance(t, l, g):
                if l == 0:
                    dve.wait_ge(*x_loaded(t, g, 16))
                else:
                    dve.wait_ge(*W.emptied(t, ("xT", 0)))
                for k in range(NBLK):
                    dve.bn_stats(ln_stat[l][:, k, :], ln_src[l][:, k, :]).then_inc(stat_done[l].sem, 1)
                for k in range(NBLK):
                    stats = stat_done[l](t, g, k + 1)
                    dve.wait_ge(first_in, N_FIRST)
                    dve.wait_ge(*stats)
                    dve.bn_aggr(ln_mv[l][:, k, :], ln_stat[l][:, k, :]).then_inc(aggr_done[l].sem, 1)
                dve.wait_ge(*aggr_done[l](t, g, NBLK))
                dve.tensor_scalar(ln_var[l][:], ln_mv[l][:, :, 1], EPS, None, ALU.add).then_inc(var_done[l].sem, 1)

            def ln_apply(t, l, g):
                dve.wait_ge(*rstd_done[l](t, g))
                if l == 1 and t.has(-1):
                    dve.wait_ge(*W.filled(t, ("xnT", 0)))
                for k in range(NBLK):
                    ins = dve.tensor_scalar(xn[:, k, :], ln_src[l][:, k, :], ln_mv[l][:, k, 0:1], ln_rstd[l][:, k:k + 1],
                                            ALU.subtract, ALU.mult)
                ins.then_inc(xn_done[l].sem, 1)

            def gate_stage(t, l, g, stage):
                count = [0 if stage == 0 else 2 + sum(GATE_LINKS[:stage - 1])]

                def link(ins):
                    count[0] += 1
                    ins.then_inc(gate_step[l].sem, 1)
                    dve.wait_ge(*gate_step[l](t, g, count[0]))

                def first_max(src, mx, vmx, onehot):
                    link(dve.tensor_reduce(mx[:], src[:], AX.X, ALU.max))
                    link(dve.tensor_tensor(lg["eq"][:], src[:], over_experts(mx), ALU.is_equal))
                    link(dve.tensor_tensor(lg["val"][:], lg["eq"][:], rank_s[:], ALU.mult))
                    link(dve.tensor_reduce(vmx[:], lg["val"][:], AX.X, ALU.max))
                    link(dve.tensor_tensor(onehot[:], lg["val"][:], over_experts(vmx), ALU.is_equal))

                if stage == 0:
                    step = ("gate", l)
                    dve.wait_ge(*W.filled(t, step))
                    dve.tensor_copy(lg["logit"][:], W.bank(t, step)[:, 0:NBLK * E].rearrange("p (k e) -> p k e", e=E))\
                       .then_inc(W.free_sem(t, step), 1)
                    dve.wait_ge(*W.emptied(t, step))
                    if l == 0:
                        first_max(lg["logit"], lgs["max"], lgs["vmax"], weight[0])
                    else:
                        link(dve.tensor_reduce(lgs["max"][:], lg["logit"][:], AX.X, ALU.max))
                        link(dve.tensor_tensor(g_shift[:], lg["logit"][:], over_experts(lgs["max"]), ALU.subtract))
                elif stage == 1:
                    dve.wait_ge(*gate_exp(t, g))
                    link(dve.tensor_reduce(lgs["sum"][:], lg["exp"][:], AX.X, ALU.add))
                    link(dve.reciprocal(lgs["rsum"][:], lgs["sum"][:]))
                    link(dve.tensor_tensor(lg["prob"][:], lg["exp"][:], over_experts(lgs["rsum"]), ALU.mult))
                elif stage == 2:
                    first_max(lg["prob"], lgs["max"], lgs["vmax"], lg["oh1"])
                elif stage == 3:
                    link(dve.scalar_tensor_tensor(out=lg["prob2"][:], in0=lg["oh1"][:], scalar=-2.0, in1=lg["prob"][:],
                                                  op0=ALU.mult, op1=ALU.add))
                    first_max(lg["prob2"], lgs["max2"], lgs["vmax2"], lg["oh2"])
                else:
                    link(dve.tensor_tensor(lg["both"][:], lg["oh1"][:], lg["oh2"][:], ALU.add))
                    link(dve.tensor_tensor(lg["prob2"][:], lg["prob"][:], lg["both"][:], ALU.mult))
                    link(dve.tensor_reduce(lgs["csum"][:], lg["prob2"][:], AX.X, ALU.add))
                    link(dve.reciprocal(lgs["rcsum"][:], lgs["csum"][:]))
                    link(dve.tensor_tensor(weight[1][:], lg["prob2"][:], over_experts(lgs["rcsum"]), ALU.mult))
                if l == 1 and stage > 0:
                    assert count[0] == 2 + sum(GATE_LINKS[:stage])

            def steps(t):
                for step in t.seg.steps:
                    kind, l, g = step[0], step[1], lag(step)
                    if t.seg.first == -1 and step == ("proj", 0, "q"):
                        set_up_scores()
                    if kind == "ln":
                        ln_variance(t, l, g)
                    elif kind == "xn":
                        ln_apply(t, l, g)
                    elif kind == "proj" and l == 0:
                        name, rotated = step[2][0], len(step[2]) == 2
                        if step[2] == "q" and t.has(g + 2):
                            dve.wait_ge(*lo_done[1](t, g + 2, 2))
                        dve.wait_ge(*W.filled(t, step))
                        dve.tensor_tensor((rope_b if rotated else rope_a)[name][:], W.bank(t, step)[:],
                                          (sin_s if rotated else cos_s)[:], ALU.mult).then_inc(W.free_sem(t, step), 1)
                    elif kind == "gate":
                        gate_stage(t, l, g, 0)
                    elif kind == "gate2":
                        gate_stage(t, l, g, step[2] + 1)
                    elif kind == "v" and l == 1:
                        if t.has(g + 1):
                            dve.wait_ge(*pv_done[1](t, g + 1, GROUPS))
                        dve.wait_ge(*W.filled(t, step))
                        dve.tensor_tensor(v_ext[1][:, :, :, 0:DK], W.bank(t, step)[:].rearrange("p (k h d) -> p k h d", k=NBLK, h=HEADS),
                                          bv_s[:].rearrange("p (o h d) -> p o h d", o=1, h=HEADS).to_broadcast([P, NBLK, HEADS, DK]),
                                          ALU.add).then_inc(W.free_sem(t, step), 1)
                    elif kind == "s":
                        p, j, qb = step[2:]
                        grp = p // 2
                        if p % 2 == 0 and j == 0 and qb == 0:
                            for l2, grp2, g2 in before_group(t, l, grp, g):
                                dve.wait_ge(*neg_step[l2](t, g2, 4 * (grp2 + 1)))
                        dve.wait_ge(*S.filled(t, step))
                        n, sides = keys_of(l, qb), sides_in_bank(l, qb)
                        dve.tensor_reduce(neg_max[grp % 2][:, j:j + sides, p % 2, qb],
                                          S.bank(t, step)[:, 0:n * sides].rearrange("p (j n) -> p j n", j=sides),
                                          AX.X, ALU.max, negate=True).then_inc(S.free_sem(t, step), 1)
                    elif kind == "silu":
                        if l == 0:
                            dve.wait_ge(*y0_step(t, g, E))
                            dve.tensor_tensor(g_s[0][:], y_ps[:], xnT[0][:], ALU.add).then_inc(y_read.sem, 1)
                    elif kind == "gmul":
                        dve.wait_ge(*tanh_done[l](t, g))
                        dve.tensor_scalar(y_sig[:], y_sig[:], 0.5, 0.5, ALU.mult, ALU.add).then_inc(sig_done[l].sem, 1)
                        if l == 1:
                            dve.wait_ge(*sig_done[1](t, g))
                            dve.tensor_tensor(g_s[1][:], y_ps[:], y_sig[:], ALU.mult).then_inc(g_done[1].sem, 1)
                    elif kind == "rcp":
                        c = step[2]
                        if c == 0:
                            dve.wait_ge(*o_moved[l](t, g, 16 * 8))
                        part = o_den[l][:, P * c:P * c + P]
                        dve.reciprocal(part, part).then_inc(rcp_done[l].sem, 1)
                    elif kind == "wo":
                        dve.wait_ge(*g_done[l](t, g))
                        dve.wait_ge(*W.filled(t, step))
                        if l == 0:
                            dve.tensor_tensor(g_s[0][:], W.bank(t, step)[:], g_s[0][:], ALU.mult).then_inc(W.free_sem(t, step), 1)
                        else:
                            dve.scalar_tensor_tensor(out=g_s[1][:], in0=W.bank(t, step)[:], scalar=bo_s[:, 0:1], in1=g_s[1][:],
                                                     op0=ALU.add, op1=ALU.mult).then_inc(W.free_sem(t, step), 1)
                    elif kind == "xT":
                        dve.wait_ge(*W.filled(t, step))
                        if l == 1:
                            dve.wait_ge(*out_stored(t, g, 0))
                            dve.wait_ge(*held(t, g))
                        else:
                            dve.wait_ge(*kept(t, g))
                        if l == 0 and t.has(1):
                            dve.wait_ge(*held(t, 1))
                        dve.tensor_tensor((x_mid, x_out)[l][:], W.bank(t, step)[:].rearrange("p (k d) -> p k d", k=NBLK),
                                          (x_keep, x_hold)[l][:], ALU.add).then_inc(W.free_sem(t, step), 1)

            for seg in SEGMENTS:
                with iterations(dve, seg, (1, 2, NBLK, E, GATE_OPS[0], GATE_OPS[1], 16, 4 * GROUPS, 16 * 8), ("work", "score")) as turn:
                    steps(turn)

        @block.gpsimd
        def _(pool):
            for tile in (k_ext[0], q_ext[0][0], q_ext[0][1]):
                nc.gpsimd.memset(tile[:].rearrange("p h n -> p (h n)").bitcast(F32), 0.0).then_inc(zeroed, 1)
            for l in LAYERS:
                nc.gpsimd.memset(v_ext[l][:], 1.0).then_inc(ones_set, 1)
            pool.wait_ge(first_in, N_FIRST)

            def steps(t):
                for step in t.seg.steps:
                    kind, l, g = step[0], step[1], lag(step)
                    if kind == "ln":
                        if t.seg.first == -1:
                            pool.wait_ge(consts_cast, 1)
                        pool.wait_ge(*var_done[l](t, g))
                        nc.gpsimd.tensor_tensor(ln_rstd[l][:], ln_var[l][:], neg_half[:], ALU.pow).then_inc(rstd_done[l].sem, 1)
                    elif kind == "proj" and len(step[2]) == 2:
                        name = step[2][0]
                        pool.wait_ge(*W.emptied(t, ("proj", 0, name)))
                        pool.wait_ge(*W.emptied(t, step))
                        if name == "q" and t.has(1):
                            pool.wait_ge(*hi_done[1](t, 1, 2))
                        nc.gpsimd.tensor_tensor(full[name][:], rope_a[name][:], rope_b[name][:], ALU.add).then_inc(full_done.sem, 1)
                    elif kind == "hi":
                        i = "qk".index(step[2])
                        pool.wait_ge(*hi_done[l](t, g, i + 1))
                        nc.gpsimd.tensor_tensor(rest[step[2]][:], full[step[2]][:], parts[step[2]][:, 0, :], ALU.subtract)\
                          .then_inc(rest_done[l].sem, 1)
                    elif kind == "mid":
                        i = "qk".index(step[2])
                        pool.wait_ge(*mid_done[l](t, g, i + 1))
                        nc.gpsimd.tensor_tensor(parts[step[2]][:, 2, :], rest[step[2]][:], parts[step[2]][:, 1, :], ALU.subtract)\
                          .then_inc(lo_done[l].sem, 1)
                    elif kind == "neg":
                        grp = step[2]
                        i, k = grp % 2, 4 * grp
                        rows_gone = [mrow_in[l2][i](t, g2, 32 * (grp2 // 2 + 1)) for l2, grp2, g2 in before_group(t, l, grp, g)]
                        maxima = S.emptied(t, ("s", l, 2 * grp + 1, 1, NBLK - 1))
                        pool.wait_ge(first_in, N_FIRST)
                        for wait in rows_gone:
                            pool.wait_ge(*wait)
                        pool.wait_ge(*maxima)
                        nc.gpsimd.tensor_copy(neg3[i][:, :, 0, :, :], neg_max[i][:]).then_inc(neg_step[l].sem, 1)
                        pool.wait_ge(*neg_step[l](t, g, k + 1))
                        nc.gpsimd.tensor_tensor(neg_rest[i][:], neg_max[i][:], neg3[i][:, :, 0, :, :], ALU.subtract)\
                          .then_inc(neg_step[l].sem, 1)
                        rests = neg_step[l](t, g, k + 2)
                        pool.wait_ge(first_in, N_FIRST)
                        pool.wait_ge(*rests)
                        nc.gpsimd.tensor_copy(neg3[i][:, :, 1, :, :], neg_rest[i][:]).then_inc(neg_step[l].sem, 1)
                        pool.wait_ge(*neg_step[l](t, g, k + 3))
                        nc.gpsimd.tensor_tensor(neg3[i][:, :, 2, :, :], neg_rest[i][:], neg3[i][:, :, 1, :, :], ALU.subtract)\
                          .then_inc(neg_step[l].sem, 1)
                    elif kind == "keep":
                        there = [x_loaded(t, g, 16)]
                        if t.has(g + 1):
                            there += [W.emptied(t, ("xT", 0))]
                        pool.wait_ge(first_in, N_FIRST)
                        for wait in there:
                            pool.wait_ge(*wait)
                        nc.gpsimd.tensor_copy(x_keep[:], x_in[:]).then_inc(kept.sem, 1)
                    elif kind == "hold":
                        there = [xn_done[1](t, g)]
                        if t.has(g + 1):
                            there += [W.emptied(t, ("xT", 1))]
                        pool.wait_ge(first_in, N_FIRST)
                        for wait in there:
                            pool.wait_ge(*wait)
                        nc.gpsimd.tensor_copy(x_hold[:], x_mid[:]).then_inc(held.sem, 1)
                    elif kind == "st" and l == 0 and step[3] == 3:
                        kb = step[4]
                        exps = T.emptied(t, step)
                        pool.wait_ge(first_in, N_FIRST)
                        pool.wait_ge(*exps)
                        v = probs[:, kb, :, P * kb:P * kb + P]
                        nc.gpsimd.affine_select(out=v, in_=v, compare_op=ALU.is_ge, fill=0.0, base=0,
                                                pattern=[[0, 4], [1, P]], channel_multiplier=-1).then_inc(mask_done.sem, 1)
                    elif kind == "xe":
                        e = step[2]
                        for l2, e2, g2 in before_expert(t, l, e, g, XE):
                            if l2 == 0:
                                pool.wait_ge(*y0_step(t, g2, e2 + 1))
                            elif g2 == lag(("h", 1, e2, NF - 1)):
                                pool.wait_ge(*W.filled(t, ("h", 1, e2, NF - 1)))
                            else:
                                pool.wait_ge(*y_full(t, g2))
                        pool.wait_ge(*spread_in[l][e % SPREAD](t, g, 16 * (e // SPREAD + 1)))
                        nc.gpsimd.tensor_tensor(x_e[e % XE][:], xnT[l][:], spread_w[e % SPREAD][:], ALU.mult)\
                          .then_inc(xe_done[l].sem, 1)
                    elif kind == "nrm":
                        pool.wait_ge(*rcp_done[l](t, g, NBLK))
                        nc.gpsimd.tensor_tensor(o_heads[l][:], o_heads[l][:], o_den[l][:], ALU.mult).then_inc(nrm_done[l].sem, 1)
                    elif kind == "gmul" and l == 0:
                        pool.wait_ge(*sig_done[0](t, g))
                        nc.gpsimd.tensor_tensor(g_s[0][:], g_s[0][:], y_sig[:], ALU.mult).then_inc(g_done[0].sem, 1)

            for seg in SEGMENTS:
                with iterations(pool, seg, (1, 2, NBLK, E, 16, 16 * E // SPREAD, 4 * GROUPS, 16 * GROUPS)) as turn:
                    steps(turn)


_ORDER = ["x", "wq0", "wq0r", "wk0", "wk0r", "wv0", "wo0", "gate0", "expert0", "wq1", "wk1", "wv1", "wo1", "gate1",
          "w1", "w2", "bq1", "bk1", "bv1", "bo1", "slopes", "cos_t", "sin_t", "ident", "causal", "rank",
          "key_rows"]


def kernel(**inputs):
    import numpy as np
    import concourse.bacc as bacc
    from concourse.bass_utils import run_bass_kernel_spmd as run

    a = {k: np.asarray(v) for k, v in inputs.items()}

    def shaped(v):
        return np.ascontiguousarray(v)

    qk = np.array([(2 * p + j) * DK + d for j in range(2) for d in range(DK) for p in range(PAIRS)])
    swap = np.array([(2 * p + j) * DK + (d ^ 1) for j in range(2) for d in range(DK) for p in range(PAIRS)])
    oo = np.array([(4 * g + m) * DK + d for m in range(4) for d in range(DK) for g in range(GROUPS)])
    ins = {"x": shaped(a["L0_attn_x"].reshape(BATCH, NBLK, P, D).transpose(0, 2, 1, 3))}
    for l in LAYERS:
        t = f"L{l}_attn_"
        ins[f"wq{l}"] = shaped(a[t + "Wq"][qk].T)
        ins[f"wk{l}"] = shaped(a[t + "Wk"][qk].T)
        ins[f"wv{l}"] = shaped(a[t + "Wv"].T)
        ins[f"wo{l}"] = shaped(a[t + "Wo"].T[oo])
    ins["wq0r"] = shaped(a["L0_attn_Wq"][swap].T)
    ins["wk0r"] = shaped(a["L0_attn_Wk"][swap].T)
    ins["gate0"] = shaped(a["L0_ffn_gate_w"].T)
    ins["gate1"] = shaped(a["L1_ffn_Wg"])
    ins["expert0"] = shaped(a["L0_ffn_expert_w"].transpose(2, 0, 1))
    ins["w1"] = shaped(a["L1_ffn_W1"].transpose(1, 0, 2))
    ins["w2"] = shaped(a["L1_ffn_W2"].reshape(E, NF, P, D).transpose(2, 0, 1, 3))
    ins["bq1"] = shaped(a["L1_attn_bq"][qk][:, None])
    ins["bk1"] = shaped(a["L1_attn_bk"][qk][:, None])
    ins["bv1"] = shaped(np.broadcast_to(a["L1_attn_bv"][None, :], (P, D)))
    ins["bo1"] = shaped(a["L1_attn_bo"][:, None])
    ins["slopes"] = shaped(a["L1_attn_slopes"].reshape(PAIRS, 2).T.reshape(HEADS, 1))

    half = DK // 2
    inv_freq = np.float32(10000.0) ** (-np.arange(half, dtype=np.float32) * np.float32(2.0) / np.float32(DK))
    angles = np.arange(SEQ, dtype=np.float32)[None, :] * inv_freq.astype(np.float32)[:, None]
    d_of = np.array([d for j in range(2) for d in range(DK) for p in range(PAIRS)])
    sign = np.where(d_of % 2 == 0, -1.0, 1.0).astype(np.float32)[:, None]
    ins["cos_t"] = shaped(np.cos(angles.astype(np.float64)).astype(np.float32)[d_of // 2])
    ins["sin_t"] = shaped(np.sin(angles.astype(np.float64)).astype(np.float32)[d_of // 2] * sign)
    ins["ident"] = np.eye(P, dtype=np.float32)
    r = np.arange(P)
    ins["causal"] = np.where(r[None, :] > r[:, None], np.float32(MASKED), np.float32(0))
    ins["rank"] = shaped(np.broadcast_to((E - np.arange(E)).astype(np.float32), (P, NBLK, E)))
    dist = np.arange(SEQ) - (SEQ - 1)
    far = (dist // P) * P
    rows = [far] * 3 + [dist - far] * 3 + [np.ones(SEQ)] * 3
    ins["key_rows"] = np.stack(rows).astype(np.float32)

    nc = bacc.Bacc("TRN2", target_bir_lowering=False, num_devices=1)
    args = [nc.dram_tensor(f"in_{n}", ins[n].shape, F32, kind="ExternalInput").ap() for n in _ORDER]
    out = nc.dram_tensor("out", (BATCH, P, NBLK, D), F32, kind="ExternalOutput").ap()
    two_layer_kernel(nc, *args, out)
    r = run(nc, [{f"in_{n}": ins[n] for n in _ORDER}], core_ids=[0])
    y = r.results[0]["out"]
    return np.ascontiguousarray(y.transpose(0, 2, 1, 3).reshape(BATCH, SEQ, D))
```
